# Optimizing a Trainium2 kernel written in Bass

```python
import numpy as np
import jax
import jax.numpy as jnp

def _softmax(x, axis=-1):
    return jax.nn.softmax(x, axis=axis)

def _gelu(x):
    return jax.nn.gelu(x, approximate=True)

def _silu(x):
    return jax.nn.silu(x)

def _sigmoid(x):
    return jax.nn.sigmoid(x)

def _layernorm(x, axis=-1, eps=1e-05):
    m = jnp.mean(x, axis=axis, keepdims=True)
    v = jnp.var(x, axis=axis, keepdims=True)
    return (x - m) / jnp.sqrt(v + eps)

def _scatter_add(tgt, idx, src, axis=0):
    return tgt.at[idx].add(src)

def _segment_sum(src, seg, n):
    return jax.ops.segment_sum(src, seg, n)
kernel_name = 'mk_gps_d2_gnn_r8_f89f3c'

def setup_inputs(seed: int=0):
    np.random.seed(seed)
    _w = jnp.asarray

    def _rec_inputs():
        import jax
        import jax.numpy as jnp
        _gk = jax.random.key(seed)
        x = -8.776e-05 + 1 * jax.random.normal(jax.random.fold_in(_gk, 1), (1250, 512), jnp.float32)
        _s = jax.random.randint(jax.random.fold_in(_gk, 2), (10000,), 0, 1250, jnp.int32)
        _d = jax.random.randint(jax.random.fold_in(_gk, 3), (10000,), 0, 1250, jnp.int32)
        _loop = jnp.arange(1250, dtype=jnp.int32)
        src = jnp.concatenate([_s, _d, _loop])
        dst = jnp.concatenate([_d, _s, _loop])
        _o = jnp.argsort(dst, stable=True)
        src = src[_o]
        dst = dst[_o]
        edge_weight = -0.00121341 + 0.998923 * jax.random.normal(jax.random.fold_in(_gk, 13), (21250,), jnp.float32)
        return (x, src, dst, edge_weight)
    x, src, dst, edge_weight = _rec_inputs()

    def _L0_gnn_setup():
        import jax, jax.numpy as jnp
        import numpy as np
        N = 1250
        E = 20000
        D = 512
        EPS = 1e-05

        def _lin_params(key, out_d, in_d, bias=True):
            k1, k2 = jax.random.split(key)
            s = 1.0 / np.sqrt(in_d)
            W = jax.random.uniform(k1, (out_d, in_d), jnp.float32, -s, s)
            if bias:
                b = jax.random.uniform(k2, (out_d,), jnp.float32, -s, s)
                return (W, b)
            return (W,)

        def _sage_conv(x, src, dst, Wp, bp, Wl, bl, Wr):
            h = jax.nn.relu(x @ Wp.T + bp)
            agg = jax.ops.segment_sum(h[src], dst, num_segments=N)
            cnt = jax.ops.segment_sum(jnp.ones((src.shape[0],), x.dtype), dst, num_segments=N)
            agg = agg / jnp.maximum(cnt, 1.0)[:, None]
            return agg @ Wl.T + bl + x @ Wr.T

        def _relu_ln(x, g, b):
            x = jax.nn.relu(x)
            mu = jnp.mean(x, axis=-1, keepdims=True)
            var = jnp.mean(jnp.square(x - mu), axis=-1, keepdims=True)
            return (x - mu) * jax.lax.rsqrt(var + EPS) * g + b
        key = jax.random.key(seed)
        ks = jax.random.split(key, 16)
        inp = {'x': jax.random.normal(ks[0], (N, D), jnp.float32), 'edge_index': jax.random.randint(ks[1], (2, E), 0, N, jnp.int64)}
        ki = 2
        for l in range(3):
            Wp, bp = _lin_params(ks[ki], D, D)
            ki += 1
            Wl, bl = _lin_params(ks[ki], D, D)
            ki += 1
            Wr, = _lin_params(ks[ki], D, D, bias=False)
            ki += 1
            inp[f'Wp{l}'] = Wp
            inp[f'bp{l}'] = bp
            inp[f'Wl{l}'] = Wl
            inp[f'bl{l}'] = bl
            inp[f'Wr{l}'] = Wr
            if l < 2:
                inp[f'g{l}'] = jnp.ones((D,), jnp.float32)
                inp[f'be{l}'] = jnp.zeros((D,), jnp.float32)
        return inp
    _L0_gnn_all = _L0_gnn_setup()
    _L0_gnn_in = {k: v for k, v in _L0_gnn_all.items() if k in ('Wp0', 'bp0', 'Wl0', 'bl0', 'Wr0', 'g0', 'be0', 'Wp1', 'bp1', 'Wl1', 'bl1', 'Wr1', 'g1', 'be1', 'Wp2', 'bp2', 'Wl2', 'bl2', 'Wr2')}
    del _L0_gnn_all

    def _L0_mix_setup():
        import jax, jax.numpy as jnp
        import numpy as np
        H = 8
        EPS_Z = 1e-06
        LN_EPS = 1e-05

        def _ln(x, g, b):
            m = x.mean(-1, keepdims=True)
            v = ((x - m) ** 2).mean(-1, keepdims=True)
            return (x - m) * jax.lax.rsqrt(v + LN_EPS) * g + b
        key = jax.random.key(seed)
        ks = jax.random.split(key, 8)
        B, S, E, F = (4, 1024, 512, 256)
        s = 0.02
        return {'src': jax.random.normal(ks[0], (B, S, E), jnp.float32), 'Wq': jax.random.normal(ks[1], (E, E), jnp.float32) * s, 'bq': jnp.zeros((E,), jnp.float32), 'Wk': jax.random.normal(ks[2], (E, E), jnp.float32) * s, 'bk': jnp.zeros((E,), jnp.float32), 'Wv': jax.random.normal(ks[3], (E, E), jnp.float32) * s, 'bv': jnp.zeros((E,), jnp.float32), 'Wo': jax.random.normal(ks[4], (E, E), jnp.float32) * s, 'bo': jnp.zeros((E,), jnp.float32), 'W1': jax.random.normal(ks[5], (E, F), jnp.float32) * s, 'b1': jnp.zeros((F,), jnp.float32), 'W2': jax.random.normal(ks[6], (F, E), jnp.float32) * s, 'b2': jnp.zeros((E,), jnp.float32), 'g1': jnp.ones((E,), jnp.float32), 'be1': jnp.zeros((E,), jnp.float32), 'g2': jnp.ones((E,), jnp.float32), 'be2': jnp.zeros((E,), jnp.float32)}
    _L0_mix_all = _L0_mix_setup()
    _L0_mix_in = {k: v for k, v in _L0_mix_all.items() if k in ('Wq', 'bq', 'Wk', 'bk', 'Wv', 'bv', 'Wo', 'bo', 'W1', 'b1', 'W2', 'b2', 'g1', 'be1', 'g2', 'be2')}
    del _L0_mix_all

    def _L0_ffn_setup():
        import jax, jax.numpy as jnp
        import numpy as np
        K = 2
        key = jax.random.key(seed)
        ks = jax.random.split(key, 6)
        B, T, d, E, dff = (2, 256, 512, 8, 256)
        x = jax.random.normal(ks[0], (B, T, d), dtype=jnp.float32)
        Wg = jax.random.normal(ks[1], (d, E), dtype=jnp.float32) * 0.02
        W1 = jax.random.normal(ks[2], (E, d, dff), dtype=jnp.float32) * 0.02
        b1 = jnp.zeros((E, dff), dtype=jnp.float32)
        W2 = jax.random.normal(ks[3], (E, dff, d), dtype=jnp.float32) * 0.02
        b2 = jnp.zeros((E, d), dtype=jnp.float32)
        return {'x': x, 'Wg': Wg, 'W1': W1, 'b1': b1, 'W2': W2, 'b2': b2}
    _L0_ffn_all = _L0_ffn_setup()
    _L0_ffn_in = {k: v for k, v in _L0_ffn_all.items() if k in ('Wg', 'W1', 'b1', 'W2', 'b2')}
    del _L0_ffn_all

    def _L1_gnn_setup():
        import jax, jax.numpy as jnp
        import numpy as np
        N = 2500
        E = 25000
        D = 512
        H = 512

        def _layernorm(x, gamma, beta, eps=1e-05):
            mu = jnp.mean(x, axis=-1, keepdims=True)
            var = jnp.mean((x - mu) ** 2, axis=-1, keepdims=True)
            return (x - mu) * jax.lax.rsqrt(var + eps) * gamma + beta
        key = jax.random.key(seed)
        ks = jax.random.split(key, 12)
        s = 0.02
        return {'source_features': jax.random.normal(ks[0], (N, D), jnp.float32), 'weighting_gate': jax.random.normal(ks[1], (E,), jnp.float32), 'rel_pair_idx': jax.random.randint(ks[2], (E, 2), 0, N, dtype=jnp.int32), 'Wm': jax.random.normal(ks[3], (D, D // 2), jnp.float32) * s, 'bm': jnp.zeros((D // 2,), jnp.float32), 'W1': jax.random.normal(ks[4], (D, D // 4), jnp.float32) * s, 'b1': jnp.zeros((D // 4,), jnp.float32), 'gamma': jnp.ones((D // 4,), jnp.float32), 'beta': jnp.zeros((D // 4,), jnp.float32), 'W2': jax.random.normal(ks[5], (D // 4, H), jnp.float32) * s, 'b2': jnp.zeros((H,), jnp.float32)}
    _L1_gnn_all = _L1_gnn_setup()
    _L1_gnn_in = {k: v for k, v in _L1_gnn_all.items() if k in ('Wm', 'bm', 'W1', 'b1', 'gamma', 'beta', 'W2', 'b2')}
    del _L1_gnn_all

    def _L1_mix_setup():
        import jax, jax.numpy as jnp
        import numpy as np
        B, N, C = (4, 1024, 512)
        H, D = (8, 64)
        EPS = 1e-06
        key = jax.random.key(seed)
        k1, k2, k3 = jax.random.split(key, 3)
        x = jax.random.normal(k1, (B, N, C), dtype=jnp.float32)
        W_qkv = jax.random.normal(k2, (3 * H * D, C), dtype=jnp.float32) * C ** (-0.5)
        W_proj = jax.random.normal(k3, (C, H * D), dtype=jnp.float32) * (H * D) ** (-0.5)
        b_proj = jnp.zeros((C,), dtype=jnp.float32)
        return {'x': x, 'W_qkv': W_qkv, 'W_proj': W_proj, 'b_proj': b_proj}
    _L1_mix_all = _L1_mix_setup()
    _L1_mix_in = {k: v for k, v in _L1_mix_all.items() if k in ('W_qkv', 'W_proj', 'b_proj')}
    del _L1_mix_all

    def _L1_ffn_setup():
        import math
        import jax, jax.numpy as jnp
        import numpy as np
        B, T, D, FF, E = (32, 1024, 512, 256, 8)
        CAPACITY_FACTOR = 1.25
        CAP = int(math.ceil(CAPACITY_FACTOR * B * T / E))

        def _bank_residual(x2, Wr, br, W1, b1, W2, b2):
            N, d = x2.shape
            e = Wr.shape[1]
            logits = x2 @ Wr + br
            probs = jax.nn.softmax(logits, axis=-1)
            expert = jnp.argmax(probs, axis=-1)
            gate = jnp.take_along_axis(probs, expert[:, None], axis=-1)[:, 0]
            oneh = jax.nn.one_hot(expert, e, dtype=x2.dtype)
            pos = (jnp.cumsum(oneh, axis=0) * oneh).sum(-1).astype(jnp.int32) - 1
            keep = pos < CAP
            slot = expert.astype(jnp.int32) * CAP + jnp.minimum(pos, CAP - 1)
            xd = jnp.where(keep[:, None], x2, 0.0)
            buf = jnp.zeros((e * CAP, d), x2.dtype).at[slot].add(xd)
            buf = buf.reshape(e, CAP, d)
            h = jax.nn.gelu(jnp.einsum('ecd,edf->ecf', buf, W1) + b1[:, None, :], approximate=False)
            out = jnp.einsum('ecf,efd->ecd', h, W2) + b2[:, None, :]
            y = out.reshape(e * CAP, d)[slot]
            return y * (gate * keep.astype(x2.dtype))[:, None]
        key = jax.random.key(seed)
        ks = jax.random.split(key, 18)
        s = 0.02
        inp = {'x': jax.random.normal(ks[0], (B, T, D), dtype=jnp.float32), 'Wr_sp': jax.random.normal(ks[1], (D, E)) * s, 'br_sp': jnp.zeros((E,), jnp.float32), 'Wr_fq': jax.random.normal(ks[2], (D, E)) * s, 'br_fq': jnp.zeros((E,), jnp.float32), 'Ws1': jax.random.normal(ks[3], (D, FF)) * s, 'bs1': jnp.zeros((FF,), jnp.float32), 'Ws2': jax.random.normal(ks[4], (FF, D)) * s, 'bs2': jnp.zeros((D,), jnp.float32), 'W1_sp': jax.random.normal(ks[5], (E, D, FF)) * s, 'b1_sp': jnp.zeros((E, FF), jnp.float32), 'W2_sp': jax.random.normal(ks[6], (E, FF, D)) * s, 'b2_sp': jnp.zeros((E, D), jnp.float32), 'W1_fq': jax.random.normal(ks[7], (E, D, FF)) * s, 'b1_fq': jnp.zeros((E, FF), jnp.float32), 'W2_fq': jax.random.normal(ks[8], (E, FF, D)) * s, 'b2_fq': jnp.zeros((E, D), jnp.float32)}
        return inp
    _L1_ffn_all = _L1_ffn_setup()
    _L1_ffn_in = {k: v for k, v in _L1_ffn_all.items() if k in ('Wr_sp', 'br_sp', 'Wr_fq', 'br_fq', 'Ws1', 'bs1', 'Ws2', 'bs2', 'W1_sp', 'b1_sp', 'W2_sp', 'b2_sp', 'W1_fq', 'b1_fq', 'W2_fq', 'b2_fq')}
    del _L1_ffn_all
    return {'x': x, 'src': src, 'dst': dst, 'edge_weight': edge_weight, 'L0_gnn_Wp0': _L0_gnn_in['Wp0'], 'L0_gnn_bp0': _L0_gnn_in['bp0'], 'L0_gnn_Wl0': _L0_gnn_in['Wl0'], 'L0_gnn_bl0': _L0_gnn_in['bl0'], 'L0_gnn_Wr0': _L0_gnn_in['Wr0'], 'L0_gnn_g0': _L0_gnn_in['g0'], 'L0_gnn_be0': _L0_gnn_in['be0'], 'L0_gnn_Wp1': _L0_gnn_in['Wp1'], 'L0_gnn_bp1': _L0_gnn_in['bp1'], 'L0_gnn_Wl1': _L0_gnn_in['Wl1'], 'L0_gnn_bl1': _L0_gnn_in['bl1'], 'L0_gnn_Wr1': _L0_gnn_in['Wr1'], 'L0_gnn_g1': _L0_gnn_in['g1'], 'L0_gnn_be1': _L0_gnn_in['be1'], 'L0_gnn_Wp2': _L0_gnn_in['Wp2'], 'L0_gnn_bp2': _L0_gnn_in['bp2'], 'L0_gnn_Wl2': _L0_gnn_in['Wl2'], 'L0_gnn_bl2': _L0_gnn_in['bl2'], 'L0_gnn_Wr2': _L0_gnn_in['Wr2'], 'L0_mix_Wq': _L0_mix_in['Wq'], 'L0_mix_bq': _L0_mix_in['bq'], 'L0_mix_Wk': _L0_mix_in['Wk'], 'L0_mix_bk': _L0_mix_in['bk'], 'L0_mix_Wv': _L0_mix_in['Wv'], 'L0_mix_bv': _L0_mix_in['bv'], 'L0_mix_Wo': _L0_mix_in['Wo'], 'L0_mix_bo': _L0_mix_in['bo'], 'L0_mix_W1': _L0_mix_in['W1'], 'L0_mix_b1': _L0_mix_in['b1'], 'L0_mix_W2': _L0_mix_in['W2'], 'L0_mix_b2': _L0_mix_in['b2'], 'L0_mix_g1': _L0_mix_in['g1'], 'L0_mix_be1': _L0_mix_in['be1'], 'L0_mix_g2': _L0_mix_in['g2'], 'L0_mix_be2': _L0_mix_in['be2'], 'L0_ffn_Wg': _L0_ffn_in['Wg'], 'L0_ffn_W1': _L0_ffn_in['W1'], 'L0_ffn_b1': _L0_ffn_in['b1'], 'L0_ffn_W2': _L0_ffn_in['W2'], 'L0_ffn_b2': _L0_ffn_in['b2'], 'L1_gnn_Wm': _L1_gnn_in['Wm'], 'L1_gnn_bm': _L1_gnn_in['bm'], 'L1_gnn_W1': _L1_gnn_in['W1'], 'L1_gnn_b1': _L1_gnn_in['b1'], 'L1_gnn_gamma': _L1_gnn_in['gamma'], 'L1_gnn_beta': _L1_gnn_in['beta'], 'L1_gnn_W2': _L1_gnn_in['W2'], 'L1_gnn_b2': _L1_gnn_in['b2'], 'L1_mix_W_qkv': _L1_mix_in['W_qkv'], 'L1_mix_W_proj': _L1_mix_in['W_proj'], 'L1_mix_b_proj': _L1_mix_in['b_proj'], 'L1_ffn_Wr_sp': _L1_ffn_in['Wr_sp'], 'L1_ffn_br_sp': _L1_ffn_in['br_sp'], 'L1_ffn_Wr_fq': _L1_ffn_in['Wr_fq'], 'L1_ffn_br_fq': _L1_ffn_in['br_fq'], 'L1_ffn_Ws1': _L1_ffn_in['Ws1'], 'L1_ffn_bs1': _L1_ffn_in['bs1'], 'L1_ffn_Ws2': _L1_ffn_in['Ws2'], 'L1_ffn_bs2': _L1_ffn_in['bs2'], 'L1_ffn_W1_sp': _L1_ffn_in['W1_sp'], 'L1_ffn_b1_sp': _L1_ffn_in['b1_sp'], 'L1_ffn_W2_sp': _L1_ffn_in['W2_sp'], 'L1_ffn_b2_sp': _L1_ffn_in['b2_sp'], 'L1_ffn_W1_fq': _L1_ffn_in['W1_fq'], 'L1_ffn_b1_fq': _L1_ffn_in['b1_fq'], 'L1_ffn_W2_fq': _L1_ffn_in['W2_fq'], 'L1_ffn_b2_fq': _L1_ffn_in['b2_fq']}

def reference(x, src, dst, edge_weight, L0_gnn_Wp0, L0_gnn_bp0, L0_gnn_Wl0, L0_gnn_bl0, L0_gnn_Wr0, L0_gnn_g0, L0_gnn_be0, L0_gnn_Wp1, L0_gnn_bp1, L0_gnn_Wl1, L0_gnn_bl1, L0_gnn_Wr1, L0_gnn_g1, L0_gnn_be1, L0_gnn_Wp2, L0_gnn_bp2, L0_gnn_Wl2, L0_gnn_bl2, L0_gnn_Wr2, L0_mix_Wq, L0_mix_bq, L0_mix_Wk, L0_mix_bk, L0_mix_Wv, L0_mix_bv, L0_mix_Wo, L0_mix_bo, L0_mix_W1, L0_mix_b1, L0_mix_W2, L0_mix_b2, L0_mix_g1, L0_mix_be1, L0_mix_g2, L0_mix_be2, L0_ffn_Wg, L0_ffn_W1, L0_ffn_b1, L0_ffn_W2, L0_ffn_b2, L1_gnn_Wm, L1_gnn_bm, L1_gnn_W1, L1_gnn_b1, L1_gnn_gamma, L1_gnn_beta, L1_gnn_W2, L1_gnn_b2, L1_mix_W_qkv, L1_mix_W_proj, L1_mix_b_proj, L1_ffn_Wr_sp, L1_ffn_br_sp, L1_ffn_Wr_fq, L1_ffn_br_fq, L1_ffn_Ws1, L1_ffn_bs1, L1_ffn_Ws2, L1_ffn_bs2, L1_ffn_W1_sp, L1_ffn_b1_sp, L1_ffn_W2_sp, L1_ffn_b2_sp, L1_ffn_W1_fq, L1_ffn_b1_fq, L1_ffn_W2_fq, L1_ffn_b2_fq):
    import jax
    import jax.numpy as jnp

    def _L0_gnn_ref(x, edge_index, Wp0, bp0, Wl0, bl0, Wr0, g0, be0, Wp1, bp1, Wl1, bl1, Wr1, g1, be1, Wp2, bp2, Wl2, bl2, Wr2):
        import jax, jax.numpy as jnp
        import numpy as np
        N = 1250
        E = 20000
        D = 512
        EPS = 1e-05

        def _lin_params(key, out_d, in_d, bias=True):
            k1, k2 = jax.random.split(key)
            s = 1.0 / np.sqrt(in_d)
            W = jax.random.uniform(k1, (out_d, in_d), jnp.float32, -s, s)
            if bias:
                b = jax.random.uniform(k2, (out_d,), jnp.float32, -s, s)
                return (W, b)
            return (W,)

        def _sage_conv(x, src, dst, Wp, bp, Wl, bl, Wr):
            h = jax.nn.relu(x @ Wp.T + bp)
            agg = jax.ops.segment_sum(h[src], dst, num_segments=N)
            cnt = jax.ops.segment_sum(jnp.ones((src.shape[0],), x.dtype), dst, num_segments=N)
            agg = agg / jnp.maximum(cnt, 1.0)[:, None]
            return agg @ Wl.T + bl + x @ Wr.T

        def _relu_ln(x, g, b):
            x = jax.nn.relu(x)
            mu = jnp.mean(x, axis=-1, keepdims=True)
            var = jnp.mean(jnp.square(x - mu), axis=-1, keepdims=True)
            return (x - mu) * jax.lax.rsqrt(var + EPS) * g + b
        src, dst = (edge_index[0], edge_index[1])
        x = _sage_conv(x, src, dst, Wp0, bp0, Wl0, bl0, Wr0)
        x = _relu_ln(x, g0, be0)
        x = _sage_conv(x, src, dst, Wp1, bp1, Wl1, bl1, Wr1)
        x = _relu_ln(x, g1, be1)
        x = _sage_conv(x, src, dst, Wp2, bp2, Wl2, bl2, Wr2)
        return x

    def _L0_mix_ref(src, Wq, bq, Wk, bk, Wv, bv, Wo, bo, W1, b1, W2, b2, g1, be1, g2, be2):
        import jax, jax.numpy as jnp
        import numpy as np
        H = 8
        EPS_Z = 1e-06
        LN_EPS = 1e-05

        def _ln(x, g, b):
            m = x.mean(-1, keepdims=True)
            v = ((x - m) ** 2).mean(-1, keepdims=True)
            return (x - m) * jax.lax.rsqrt(v + LN_EPS) * g + b
        B, S, E = src.shape
        Dh = E // H

        def heads(x):
            return x.reshape(B, S, H, Dh).transpose(0, 2, 1, 3)
        q = heads(src @ Wq + bq)
        k = heads(src @ Wk + bk)
        v = heads(src @ Wv + bv)
        qm = jax.nn.elu(q) + 1.0
        km = jax.nn.elu(k) + 1.0
        kv = jnp.einsum('bhsd,bhse->bhde', km, v)
        ksum = km.sum(axis=2)
        z = 1.0 / (jnp.einsum('bhsd,bhd->bhs', qm, ksum) + EPS_Z)
        attn = jnp.einsum('bhsd,bhde->bhse', qm, kv) * z[..., None]
        attn = attn.transpose(0, 2, 1, 3).reshape(B, S, E) @ Wo + bo
        x = _ln(src + attn, g1, be1)
        ff = jax.nn.relu(x @ W1 + b1) @ W2 + b2
        return _ln(x + ff, g2, be2)

    def _L0_ffn_ref(x, Wg, W1, b1, W2, b2):
        import jax, jax.numpy as jnp
        import numpy as np
        K = 2
        logits = jnp.einsum('btd,de->bte', x, Wg)
        probs = jax.nn.softmax(logits, axis=-1)
        top_p, _top_i = jax.lax.top_k(probs, K)
        top_p = top_p / jnp.sum(top_p, axis=-1, keepdims=True)
        b2_sum = jnp.sum(b2, axis=0)
        out = jnp.zeros_like(x)
        for i in range(K):
            w_in = x * top_p[..., i:i + 1]
            h = jax.nn.gelu(jnp.einsum('btd,edf->ebtf', w_in, W1) + b1[:, None, None, :], approximate=False)
            out = out + jnp.einsum('ebtf,efd->btd', h, W2) + b2_sum
        return out

    def _L1_gnn_ref(source_features, weighting_gate, rel_pair_idx, Wm, bm, W1, b1, gamma, beta, W2, b2):
        import jax, jax.numpy as jnp
        import numpy as np
        N = 2500
        E = 25000
        D = 512
        H = 512

        def _layernorm(x, gamma, beta, eps=1e-05):
            mu = jnp.mean(x, axis=-1, keepdims=True)
            var = jnp.mean((x - mu) ** 2, axis=-1, keepdims=True)
            return (x - mu) * jax.lax.rsqrt(var + eps) * gamma + beta
        src = rel_pair_idx[:, 0]
        dst = rel_pair_idx[:, 1]
        n_nodes = source_features.shape[0]
        m = jnp.maximum(jnp.max(weighting_gate), jnp.float32(0.0))
        exp_e = jnp.exp(weighting_gate - m)
        row_sum = jax.ops.segment_sum(exp_e, src, num_segments=n_nodes)
        atten_e = exp_e / (row_sum[src] + 1e-06)
        Mfeat = source_features @ Wm + bm
        out0 = jax.ops.segment_sum(atten_e[:, None] * Mfeat[dst], src, num_segments=n_nodes)
        out1 = jax.ops.segment_sum(atten_e[:, None] * Mfeat[src], dst, num_segments=n_nodes)
        message_feats = jnp.concatenate([out0, out1], axis=-1)
        h = message_feats @ W1 + b1
        h = jax.nn.relu(_layernorm(h, gamma, beta))
        h = jax.nn.relu(h @ W2 + b2)
        valid = (row_sum > 0)[:, None]
        return jnp.where(valid, h, jnp.float32(0.0))

    def _L1_mix_ref(x, W_qkv, W_proj, b_proj):
        import jax, jax.numpy as jnp
        import numpy as np
        B, N, C = (4, 1024, 512)
        H, D = (8, 64)
        EPS = 1e-06
        b, n, c = x.shape
        qkv = x @ W_qkv.T
        q, k, v = jnp.split(qkv, 3, axis=-1)
        to_heads = lambda t: t.reshape(b, n, H, D).transpose(0, 2, 1, 3)
        q, k, v = (to_heads(q), to_heads(k), to_heads(v))
        q = jax.nn.sigmoid(q)
        k = jax.nn.sigmoid(k)
        scale = D ** (-0.5)
        v = v / (scale * c // H)
        k_sum = k.sum(axis=2)
        q_sum = q.sum(axis=2)
        sink_incoming = 1.0 / (((q + EPS) * (k_sum + EPS)[:, :, None, :]).sum(-1) + EPS)
        source_outgoing = 1.0 / (((k + EPS) * (q_sum + EPS)[:, :, None, :]).sum(-1) + EPS)
        conserved_sink = ((q + EPS) * ((k * source_outgoing[..., None]).sum(2) + EPS)[:, :, None, :]).sum(-1) + EPS
        conserved_source = ((k + EPS) * ((q * sink_incoming[..., None]).sum(2) + EPS)[:, :, None, :]).sum(-1) + EPS
        conserved_source = jnp.clip(conserved_source, -1.0, 1.0)
        sink_allocation = jax.nn.sigmoid(conserved_sink * (float(q.shape[2]) / float(k.shape[2])))
        source_competition = jax.nn.softmax(conserved_source, axis=-1) * float(k.shape[2])
        kv = jnp.einsum('bhnd,bhne->bhde', k, v * source_competition[..., None])
        x_update = jnp.einsum('bhnd,bhde->bhne', q, kv) * sink_incoming[..., None] * sink_allocation[..., None]
        out = x_update.transpose(0, 2, 1, 3).reshape(b, n, H * D)
        return out @ W_proj.T + b_proj

    def _L1_ffn_ref(x, Wr_sp, br_sp, Wr_fq, br_fq, Ws1, bs1, Ws2, bs2, W1_sp, b1_sp, W2_sp, b2_sp, W1_fq, b1_fq, W2_fq, b2_fq):
        import math
        import jax, jax.numpy as jnp
        import numpy as np
        B, T, D, FF, E = (32, 1024, 512, 256, 8)
        CAPACITY_FACTOR = 1.25
        CAP = int(math.ceil(CAPACITY_FACTOR * B * T / E))

        def _bank_residual(x2, Wr, br, W1, b1, W2, b2):
            N, d = x2.shape
            e = Wr.shape[1]
            logits = x2 @ Wr + br
            probs = jax.nn.softmax(logits, axis=-1)
            expert = jnp.argmax(probs, axis=-1)
            gate = jnp.take_along_axis(probs, expert[:, None], axis=-1)[:, 0]
            oneh = jax.nn.one_hot(expert, e, dtype=x2.dtype)
            pos = (jnp.cumsum(oneh, axis=0) * oneh).sum(-1).astype(jnp.int32) - 1
            keep = pos < CAP
            slot = expert.astype(jnp.int32) * CAP + jnp.minimum(pos, CAP - 1)
            xd = jnp.where(keep[:, None], x2, 0.0)
            buf = jnp.zeros((e * CAP, d), x2.dtype).at[slot].add(xd)
            buf = buf.reshape(e, CAP, d)
            h = jax.nn.gelu(jnp.einsum('ecd,edf->ecf', buf, W1) + b1[:, None, :], approximate=False)
            out = jnp.einsum('ecf,efd->ecd', h, W2) + b2[:, None, :]
            y = out.reshape(e * CAP, d)[slot]
            return y * (gate * keep.astype(x2.dtype))[:, None]
        b, t, d = x.shape
        x2 = x.reshape(b * t, d)
        shared = jax.nn.gelu(x2 @ Ws1 + bs1, approximate=False) @ Ws2 + bs2
        y = shared
        y = y + _bank_residual(x2, Wr_sp, br_sp, W1_sp, b1_sp, W2_sp, b2_sp)
        y = y + _bank_residual(x2, Wr_fq, br_fq, W1_fq, b1_fq, W2_fq, b2_fq)
        return y.reshape(b, t, d)
    edge_index = jnp.stack([src, dst])
    edge_index_t = jnp.stack([src, dst], axis=1)
    xn = _layernorm(x, axis=-1)
    x = x + _L0_gnn_ref(xn, edge_index, L0_gnn_Wp0, L0_gnn_bp0, L0_gnn_Wl0, L0_gnn_bl0, L0_gnn_Wr0, L0_gnn_g0, L0_gnn_be0, L0_gnn_Wp1, L0_gnn_bp1, L0_gnn_Wl1, L0_gnn_bl1, L0_gnn_Wr1, L0_gnn_g1, L0_gnn_be1, L0_gnn_Wp2, L0_gnn_bp2, L0_gnn_Wl2, L0_gnn_bl2, L0_gnn_Wr2) + _L0_mix_ref(xn[None], L0_mix_Wq, L0_mix_bq, L0_mix_Wk, L0_mix_bk, L0_mix_Wv, L0_mix_bv, L0_mix_Wo, L0_mix_bo, L0_mix_W1, L0_mix_b1, L0_mix_W2, L0_mix_b2, L0_mix_g1, L0_mix_be1, L0_mix_g2, L0_mix_be2)[0]
    x = x + _L0_ffn_ref(_layernorm(x, axis=-1)[None], L0_ffn_Wg, L0_ffn_W1, L0_ffn_b1, L0_ffn_W2, L0_ffn_b2)[0]
    xn = _layernorm(x, axis=-1)
    x = x + _L1_gnn_ref(xn, edge_weight, edge_index_t, L1_gnn_Wm, L1_gnn_bm, L1_gnn_W1, L1_gnn_b1, L1_gnn_gamma, L1_gnn_beta, L1_gnn_W2, L1_gnn_b2) + _L1_mix_ref(xn[None], L1_mix_W_qkv, L1_mix_W_proj, L1_mix_b_proj)[0]
    x = x + _L1_ffn_ref(_layernorm(x, axis=-1)[None], L1_ffn_Wr_sp, L1_ffn_br_sp, L1_ffn_Wr_fq, L1_ffn_br_fq, L1_ffn_Ws1, L1_ffn_bs1, L1_ffn_Ws2, L1_ffn_bs2, L1_ffn_W1_sp, L1_ffn_b1_sp, L1_ffn_W2_sp, L1_ffn_b2_sp, L1_ffn_W1_fq, L1_ffn_b1_fq, L1_ffn_W2_fq, L1_ffn_b2_fq)[0]
    return x

_drawn_inputs = setup_inputs


def setup_inputs(seed=0):
    import zlib

    import numpy as np

    out = dict(_drawn_inputs(seed))
    spreads = {'L0_gnn_g0': (1.0, 0.2),
     'L0_gnn_be0': (0.0, 0.1),
     'L0_gnn_g1': (1.0, 0.2),
     'L0_gnn_be1': (0.0, 0.283),
     'L0_mix_bq': (0.0, 2.0),
     'L0_mix_bk': (0.0, 2.0),
     'L0_mix_bv': (0.0, 0.367),
     'L0_mix_bo': (0.0, 0.1),
     'L0_mix_b1': (0.0, 0.781),
     'L0_mix_b2': (0.0, 0.1),
     'L0_mix_g1': (1.0, 0.2),
     'L0_mix_be1': (0.0, 0.1),
     'L0_mix_g2': (1.0, 0.2),
     'L0_mix_be2': (0.0, 0.1),
     'L0_ffn_b1': (0.0, 0.1),
     'L0_ffn_b2': (0.0, 0.1),
     'L1_gnn_bm': (0.0, 0.542),
     'L1_gnn_b1': (0.0, 0.1),
     'L1_gnn_gamma': (1.0, 0.6),
     'L1_gnn_beta': (0.0, 0.8),
     'L1_gnn_b2': (0.0, 0.1),
     'L1_mix_b_proj': (0.0, 0.1),
     'L1_ffn_br_sp': (0.0, 0.8),
     'L1_ffn_br_fq': (0.0, 0.8),
     'L1_ffn_bs1': (0.0, 0.8),
     'L1_ffn_bs2': (0.0, 0.404),
     'L1_ffn_b1_sp': (0.0, 0.8),
     'L1_ffn_b2_sp': (0.0, 0.731),
     'L1_ffn_b1_fq': (0.0, 0.8),
     'L1_ffn_b2_fq': (0.0, 0.737)}
    factors = {'edge_weight': 3.166,
     'L0_gnn_bp0': 8.0,
     'L0_gnn_bl0': 3.104,
     'L0_gnn_bp1': 8.0,
     'L0_gnn_bl1': 3.937,
     'L0_gnn_bp2': 8.0,
     'L0_gnn_bl2': 5.013,
     'L0_mix_Wq': 8.0,
     'L0_mix_Wk': 8.0,
     'L0_mix_Wv': 8.0,
     'L0_ffn_Wg': 8.0,
     'L1_mix_W_qkv': 4.533,
     'L1_mix_W_proj': 4.448,
     'L1_ffn_Wr_sp': 4.434,
     'L1_ffn_Wr_fq': 4.449,
     'L1_ffn_W1_sp': 6.736,
     'L1_ffn_W2_sp': 6.265,
     'L1_ffn_W1_fq': 6.765,
     'L1_ffn_W2_fq': 6.359,
     'L1_ffn_Ws1': 3.07}
    for name, (base, spread) in spreads.items():
        noise = np.random.default_rng([zlib.crc32(name.encode()), seed]).standard_normal(out[name].shape)
        drawn = base * np.exp(spread * noise) if base else spread * noise
        out[name] = jnp.asarray(drawn.astype(out[name].dtype))
    for name, factor in factors.items():
        out[name] = (out[name] * factor).astype(out[name].dtype)
    return out
```

```python
from contextlib import ExitStack

import numpy as np

import concourse.bass as bass
from concourse import mybir

ALU = mybir.AluOpType
ACT = mybir.ActivationFunctionType
F32 = mybir.dt.float32
F32R = mybir.dt.float32r
BF16 = mybir.dt.bfloat16
I32 = mybir.dt.int32
I16 = mybir.dt.int16
X_AXIS = mybir.AxisListType.X

N = 1250
D = 512
TP = 125
NT = N // TP
KC = D // 128
CH = [(0, 500), (500, 500), (1000, 250)]
EDGES = 21250
NCH = EDGES // TP
NPAIR = NCH // 2
BW = 32
NB = -(-N // BW)
NPAD = NB * BW
MW = N // 3 + 1
HEADS = 8
E0 = 8
E1 = 16
FF = 256
LN_EPS = 1e-5
EPS = 1e-6
UNIT = 2048

UNITS = (["mq", "mk", "mv", "mo", "mf"]
         + [f"{w}{l}" for l in range(3) for w in ("wp", "wr", "wl")]
         + [f"f{e}" for e in range(E0)]
         + ["q1", "k1", "v1", "g1", "p1", "g1b", "sh"] + [f"e{e}" for e in range(E1)])
ROWS = ["bk", "bv", "bo", "mg1", "mbe1", "mb2", "mg2", "mbe2", "bp0", "bl0", "g0", "be0",
        "bp1", "bl1", "g1", "be1", "bp2", "bl2", "gnnA", "gnnB", "gnnb2", "bproj", "bs2"]
NROW = 5
COLS = {"bq": 0, "mb1": 4, "fb1": 6, "bs1": 6 + 2 * E0, "eb1": 8 + 2 * E0}
NCOL = 8 + 2 * E0 + 2 * E1


class Counts:

    def __init__(self):
        self.full = 0
        self.free = 0
        self.a = 0
        self.d = 0
        self.stage = 0
        self.seq = 0
        self.unit = 0
        self.rows = 0
        self.dma = 0


def program(nc, A, out):
    ctx = ExitStack()
    with ctx:
        def sb(name, shape, dt=F32):
            return ctx.enter_context(nc.sbuf_tensor(name, shape, dt))

        def sem(name):
            return ctx.enter_context(nc.semaphore(name))

        d_acc = nc.dram_tensor("d_acc", [TP, NT, D], F32).ap()
        d_cnt = nc.dram_tensor("d_cnt", [TP, NT * NPAD], F32).ap()
        d_w = nc.dram_tensor("d_w", [NT, TP, NPAD], F32).ap()
        d_wt = nc.dram_tensor("d_wt", [NT, TP, N], F32).ap()

        ps = ctx.enter_context(nc.psum_tensor("ps", [128, 8, 512], F32))

        R1 = sb("R1", [128, NT * D])
        R2 = sb("R2", [128, NT * D])
        XH = sb("XH", [128, KC, N], F32R)
        XL = sb("XL", [128, KC, N], F32R)
        AR = sb("AR", [128, NT * NPAD])
        HH = sb("HH", [128, 2, N], F32R)
        HL = sb("HL", [128, 2, N], F32R)
        wraw = sb("wraw", [128, UNIT])
        wH = sb("wH", [128, 2, UNIT], F32R)
        wL = sb("wL", [128, 2, UNIT], F32R)
        V = sb("V", [128, 4, 512])
        rows = sb("rows", [128, NROW, D])
        BC = sb("BC", [128, 2, N])
        cols = sb("cols", [128, NCOL])
        wg = V[:, 0, 256:256 + KC * 24]
        wgH = sb("wgH", [128, KC, 24], F32R)
        wgL = sb("wgL", [128, KC, 24], F32R)
        ident = sb("ident", [128, 128])
        ones = sb("ones", [128, 128])
        mask_h = sb("mask_h", [128, KC, HEADS])
        mask_p = sb("mask_p", [128, 128])
        small = sb("small", [128, 936])

        R1t = R1[0:TP, :].rearrange("p (t d) -> p t d", t=NT)
        R2t = R2[0:TP, :].rearrange("p (t d) -> p t d", t=NT)
        A1 = AR[:, 0:NT * D]
        A2 = AR[:, NT * D:2 * NT * D]
        A3 = AR[:, 2 * NT * D:]
        A1t = A1[0:TP, :].rearrange("p (t d) -> p t d", t=NT)
        A2t = A2[0:TP, :].rearrange("p (t d) -> p t d", t=NT)
        A1c = A1[:, 0:KC * N].rearrange("p (k n) -> p k n", k=KC)
        A2c = A2[:, 0:KC * N].rearrange("p (k n) -> p k n", k=KC)
        CT = AR[0:TP, :].rearrange("p (t d) -> p t d", t=NT)

        _at = [0]

        def sm(k, n=1):
            a = small[:, _at[0]:_at[0] + k * n]
            _at[0] += k * n
            return a

        bnst = sm(6 * NT)
        mv = sm(2 * NT)
        std = sm(NT)
        rstd = sm(NT)
        t10 = sm(NT)
        u10 = sm(NT)
        rsum = sm(NT)
        rinv = sm(NT)
        valid = sm(NT)
        kvb = BC[:, 0, 0:512].rearrange("p (c e) -> p c e", c=KC)
        blkA = sm(KC * HEADS)
        blkB = sm(KC * HEADS)
        ksc = sm(KC)
        qsc = sm(KC)
        acc12 = sm(12)
        acc12b = sm(12)
        s80 = [sm(80) for _ in range(5)]
        lg = V[:, 2, 128:288]
        pr = sm(160)
        wtop = sm(2 * NT)
        mtop = sm(80)
        gate = sm(20)
        epsc = sm(1)
        lneps = sm(1)
        mT = BC[0:E1, 1, :]
        assert _at[0] <= 936, _at[0]
        iota8 = sb("iota8", [128, 8])
        lgs2 = V[:, 2, 0:128]
        b2f = V[:, 3, :]
        MfA = A3[0:TP, :].rearrange("p (t d) -> p t d", t=NT)
        MfB = R1[0:TP, 0:NT * 256].rearrange("p (t d) -> p t d", t=NT)
        hg = A2[0:TP, 0:NT * 128].rearrange("p (t d) -> p t d", t=NT)

        def slab_of(i):
            return (A1 if i == 0 else A2)[0:TP, 0:NT * 500].rearrange("p (t e) -> p t e", t=NT)


        stg = [R1[:, (3 * MW) * i:(3 * MW) * (i + 1)] for i in range(2)]
        wst = [R1[0:TP, 6 * MW + 1280 * i:6 * MW + 1280 * (i + 1)].rearrange("p (t e) -> p t e", t=NT) for i in range(2)]
        win = [R1[0:TP, NPAD * i:NPAD * (i + 1)] for i in range(2)]
        wout = [R2[0:TP, N * i:N * (i + 1)] for i in range(2)]
        _r2 = [0]

        def r2(k, p=128):
            a = R2[0:p, _r2[0]:_r2[0] + k]
            _r2[0] += k
            return a

        srcf = r2(NCH, TP)
        dstf = r2(NCH, TP)
        ew = r2(NCH, TP)
        exw = r2(NCH, TP)
        hbf = r2(NCH // 2, TP).bitcast(BF16)
        parts_flat = r2(4 * NCH, TP)
        parts = parts_flat.rearrange("p (c a) -> p c a", a=4)
        ohs = r2(3 * MW).bitcast(BF16).rearrange("p (i e) -> p i e", i=2)
        ohd = r2(128).bitcast(BF16).rearrange("p (i e) -> p i e", i=2)
        iota_s = r2((3 * MW + 1) // 2).bitcast(I16)[:, 0:3 * MW]
        iota_d = r2(NPAD)
        assert _r2[0] <= NT * D
        _v3 = V[:, 3, :]
        dmm = V[:, 2, 0:2 * NPAIR]
        mm2 = V[:, 2, 200:202]
        smw = V[:, 2, 204:208]
        bnd_a = V[0:NPAIR, 2, 210:210 + NB]
        bnd_b = V[0:NPAIR, 2, 260:260 + NB]
        iota_b = V[0:NPAIR, 2, 310:310 + NB]
        iota_c = V[0:NPAIR, 2, 360:362]
        bnd_v = V[:, 3, 0:2 * NB]
        bnd_c = V[:, 3, 100:101]
        bnd_f = V[:, 3, 110:110 + 2 * NB]
        bnd_i = V[:, 3, 200:200 + 2 * NB].bitcast(I32)

        max_ready = sem("max_ready")
        slab_loaded = [sem(f"slab_loaded{i}") for i in range(2)]
        pool_max = sem("pool_max")
        cnt_stored = sem("cnt_stored")
        win_loaded = [sem(f"win_loaded{i}") for i in range(2)]
        wt_stored = [sem(f"wt_stored{i}") for i in range(2)]
        psum_full = sem("psum_full")
        psum_free = sem("psum_free")
        act_out = sem("act_out")
        dve_out = sem("dve_out")
        act_seq = sem("act_seq")
        dve_seq = sem("dve_seq")
        pool_seq = sem("pool_seq")
        stage_done = sem("stage_done")
        consts_ready = sem("consts_ready")
        w_loaded = sem("w_loaded")
        w_ready = sem("w_ready")
        w_used = sem("w_used")
        rows_loaded = sem("rows_loaded")
        in_loaded = sem("in_loaded")
        act_dma = sem("act_dma")
        out_stored = sem("out_stored")
        oh_ready = sem("oh_ready")
        oh_used = sem("oh_used")
        bounds_ready = sem("bounds_ready")
        blk_full = sem("blk_full")
        blk_free = sem("blk_free")
        turn_full = sem("turn_full")
        turn_free = sem("turn_free")
        wst_full = sem("wst_full")
        wst_stored = [sem(f"wst_stored{i}") for i in range(2)]

        block = ctx.enter_context(nc.Block())

        CONSTS = 6 + 1 + 2 * (KC + 1) + 1 + 5
        def bank(j):
            return ps[:, j % 8, :]

        def end_stage(eng, n, k=3):
            n.stage += 1
            eng.drain().then_inc(stage_done, 1)
            eng.wait_ge(stage_done, 3 * n.stage)

        def row(name, w=D, o=0):
            return rows[0:TP, ROW_SLOT[name], o:o + w]

        def heads_dot(pe, n, qT, blk, eps):
            j = n.full
            pe.wait_ge(psum_free, j - 7)
            for t in range(NT):
                o = bank(j)[0:TP, 8 * t:8 * t + 8]
                for c in range(KC):
                    b = blk[:, 8 * c:8 * c + 8]
                    last = pe.matmul(o, lhsT=qT[:, c, TP * t:TP * t + TP], rhs=b, start=c == 0,
                                     stop=(eps is None and c == KC - 1), skip_group_check=True)
                if eps is not None:
                    for c in range(KC):
                        last = pe.matmul(o, lhsT=epsc.to_broadcast([128, TP]), rhs=blk[:, 8 * c:8 * c + 8], start=False,
                                         stop=c == KC - 1, skip_group_check=True)
            last.then_inc(psum_full, 1)
            n.full += 1

        def rows_attn(pe, n, qT):
            for t in range(NT):
                j = n.full
                pe.wait_ge(psum_free, j - 7)
                for c in range(KC):
                    last = pe.matmul(bank(j)[0:TP, 128 * c:128 * c + 128], lhsT=qT[:, c, TP * t:TP * t + TP],
                                     rhs=kvb[:, c, :], start=True, stop=True, skip_group_check=True)
                last.then_inc(psum_full, 1)
                n.full += 1

        def weighted_sums(pe, n, which):
            j = n.full
            pe.wait_ge(psum_free, j - 7)
            for c in range(KC):
                for t in range(NT):
                    last = pe.matmul(bank(j)[:, 8 * c:8 * c + 8], lhsT=R1t[:, t, 128 * c:128 * c + 128],
                                     rhs=s80[which][0:TP, 8 * t:8 * t + 8], start=t == 0, stop=t == NT - 1,
                                     skip_group_check=True)
            last.then_inc(psum_full, 1)
            n.full += 1

        def gate_logits(pe, n, o, w):
            j = n.full
            pe.wait_ge(psum_free, j - 7)
            for t in range(NT):
                s = slice(TP * t, TP * t + TP)
                mms = []
                for k in range(KC):
                    mms += [(XH[:, k, s], wgH[:, k, o:o + w]), (XH[:, k, s], wgL[:, k, o:o + w]),
                            (XL[:, k, s], wgH[:, k, o:o + w])]
                for i, (l, r) in enumerate(mms):
                    last = pe.matmul(bank(j)[0:TP, w * t:w * t + w], lhsT=l, rhs=r, start=i == 0,
                                     stop=i == len(mms) - 1, skip_group_check=True)
            last.then_inc(psum_full, 1)
            n.full += 1

        def graph_pe(pe, n):
            pe.wait_ge(bounds_ready, 1)
            for which in range(2):
                last = pe.transpose(ps[0:NPAIR, which, 0:TP], dmm[0:TP, NPAIR * which:NPAIR * which + NPAIR],
                                    ident[0:TP, 0:TP])
            last.then_inc(turn_full, 1)
            pe.wait_ge(bounds_ready, 2)
            pe.transpose(ps[0:2 * NB, 2, 0:NPAIR], bnd_v[0:NPAIR, :], ident[0:NPAIR, 0:NPAIR]).then_inc(turn_full, 1)
            pe.wait_ge(bounds_ready, 3)
            pe.transpose(ps[0:1, 3, 0:2 * NB], bnd_c[0:2 * NB, 0:1], ident[0:2 * NB, 0:2 * NB]).then_inc(turn_full, 1)
            pe.wait_ge(bounds_ready, 4)
            chunks = pe.alloc_register("pe_chunks")
            pe.reg_mov(chunks, 0)

            def turn_block(b):
                pe.wait_ge(blk_free, b + 1)
                for g in range(3):
                    q = 3 * b + g
                    if q >= 2:
                        pe.wait_ge(turn_free, q - 1)
                    for t in range(4 * g, min(4 * g + 4, NT)):
                        last = pe.transpose(ps[0:TP, 6 + q % 2, 128 * (t - 4 * g):128 * (t - 4 * g) + 128],
                                            stg[b % 2][:, TP * t:TP * t + TP], ident[:, :])
                    last.then_inc(turn_full, 1)

            for b in range(NB):
                lo = pe.value_load(bnd_i[0:1, NB + b:NB + b + 1], min_val=0, max_val=NPAIR - 2)
                hi = pe.value_load(bnd_i[0:1, b:b + 1], min_val=2, max_val=NPAIR)
                if b >= 2:
                    pe.wait_ge(blk_free, b - 1)

                def pair(start):
                    for i in range(2):
                        pe.wait_ge(oh_ready, pe.snap(chunks) + 1)
                        for m in range(3):
                            last = pe.matmul(ps[:, 3 * (b % 2) + m, 0:MW], lhsT=ohd[0:TP, i, :],
                                             rhs=ohs[0:TP, i, MW * m:MW * m + MW], start=(start and i == 0),
                                             stop=False, skip_group_check=True)
                        last.then_inc(oh_used, 1)
                        pe.reg_add(chunks, chunks, 1)

                pair(True)
                with pe.Fori(lo + 1, hi):
                    pair(False)
                pe.drain().then_inc(blk_full, 1)
                if b >= 1:
                    turn_block(b - 1)
            turn_block(NB - 1)

        def graph_dve(dve, n, seq):
            dve.wait_ge(act_dma, 16 * 5)
            dve.tensor_copy(srcf, V[0:TP, 0, 0:NCH].bitcast(I32)).then_inc(dve_seq, 1)
            dve.tensor_copy(dstf, V[0:TP, 1, 0:NCH].bitcast(I32)).then_inc(dve_seq, 1)
            dve.memset(parts[:, :, 0:1], 1.0).then_inc(dve_seq, 1)
            dve.tensor_reduce(smw[0:TP, 0:1], ew, X_AXIS, ALU.max).then_inc(dve_seq, 1)
            n.seq += 4
            dve.wait_ge(dve_seq, n.seq)
            dve.sem_inc(oh_used, 2)
            d2 = dstf.rearrange("p (c two) -> p c two", two=2)
            dve.tensor_reduce(dmm[0:TP, 0:NPAIR], d2, X_AXIS, ALU.min).then_inc(dve_seq, 1)
            dve.tensor_reduce(dmm[0:TP, NPAIR:2 * NPAIR], d2, X_AXIS, ALU.max).then_inc(bounds_ready, 1)
            n.seq += 1
            dve.wait_ge(turn_full, 1)
            dve.tensor_reduce(mm2[0:NPAIR, 0:1], ps[0:NPAIR, 0, 0:TP], X_AXIS, ALU.min).then_inc(dve_seq, 1)
            dve.tensor_reduce(mm2[0:NPAIR, 1:2], ps[0:NPAIR, 1, 0:TP], X_AXIS, ALU.max).then_inc(dve_seq, 1)
            n.seq += 2
            dve.wait_ge(dve_seq, n.seq)
            dve.wait_ge(consts_ready, CONSTS)
            dve.tensor_scalar(bnd_a, iota_b, mm2[0:NPAIR, 1:2], None, ALU.is_le).then_inc(dve_seq, 1)
            dve.tensor_scalar(bnd_b, iota_b, float(BW - 1), mm2[0:NPAIR, 0:1], ALU.add, ALU.is_ge)\
               .then_inc(dve_seq, 1)
            n.seq += 2
            dve.wait_ge(dve_seq, n.seq)
            dve.tensor_tensor(bnd_a, bnd_a, bnd_b, ALU.mult).then_inc(dve_seq, 1)
            n.seq += 1
            dve.wait_ge(dve_seq, n.seq)
            dve.tensor_scalar(bnd_v[0:NPAIR, 0:NB], bnd_a, iota_c[:, 0:1], None, ALU.mult).then_inc(dve_seq, 1)
            dve.tensor_scalar(bnd_v[0:NPAIR, NB:2 * NB], bnd_a, iota_c[:, 1:2], None, ALU.mult).then_inc(dve_seq, 1)
            n.seq += 2
            dve.wait_ge(dve_seq, n.seq)
            dve.sem_inc(bounds_ready, 1)
            dve.wait_ge(turn_full, 2)
            dve.tensor_reduce(bnd_c[0:2 * NB, 0:1], ps[0:2 * NB, 2, 0:NPAIR], X_AXIS, ALU.max).then_inc(bounds_ready, 1)
            dve.wait_ge(turn_full, 3)
            dve.tensor_scalar(bnd_f[0:1, NB:2 * NB], ps[0:1, 3, NB:2 * NB], -1.0, float(NPAIR), ALU.mult, ALU.add)\
               .then_inc(dve_seq, 1)
            n.seq += 1
            dve.wait_ge(dve_seq, n.seq)
            dve.tensor_scalar(bnd_f[0:1, NB:2 * NB], bnd_f[0:1, NB:2 * NB], float(NPAIR - 2), None, ALU.min)\
               .then_inc(dve_seq, 1)
            n.seq += 1
            dve.wait_ge(dve_seq, n.seq)
            dve.tensor_scalar(bnd_f[0:1, 0:NB], bnd_f[0:1, NB:2 * NB], 2.0, None, ALU.add).then_inc(dve_seq, 1)
            n.seq += 1
            dve.wait_ge(dve_seq, n.seq)
            dve.tensor_tensor(bnd_f[0:1, 0:NB], bnd_f[0:1, 0:NB], ps[0:1, 3, 0:NB], ALU.max).then_inc(dve_seq, 1)
            n.seq += 1
            dve.wait_ge(dve_seq, n.seq)
            dve.tensor_copy(bnd_i[0:1, :], bnd_f[0:1, :]).then_inc(bounds_ready, 1)
            dve.wait_ge(act_out, n.a + 1)
            p0, p1, p2 = V[0:TP, 2, 0:NCH], V[0:TP, 2, NCH:2 * NCH], V[0:TP, 3, 0:NCH]
            rest = exw
            for i in range(3):
                dve.tensor_copy(hbf, rest).then_inc(dve_seq, 1)
                n.seq += 1
                dve.wait_ge(dve_seq, n.seq)
                dve.tensor_copy(parts[:, :, 1 + i], hbf).then_inc(dve_seq, 1)
                n.seq += 1
                if i < 2:
                    dve.tensor_tensor(exw, rest, hbf, ALU.subtract).then_inc(dve_seq, 1)
                    n.seq += 1
                dve.wait_ge(dve_seq, n.seq)
            n.a += 1
            chunks = dve.alloc_register("dve_chunks")
            dve.reg_mov(chunks, 0)

            def read_block(b):
                for g in range(3):
                    q = 3 * b + g
                    dve.wait_ge(turn_full, 3 + q + 1)
                    k = min(4, NT - 4 * g)
                    o = ps[0:TP, 6 + q % 2, 0:128 * k].rearrange("p (t e) -> p t e", t=k)
                    dve.tensor_copy(CT[:, 4 * g:4 * g + k, BW * b:BW * b + BW], o[:, :, 0:BW]).then_inc(dve_seq, 1)
                    n.seq += 1
                    if b % 4 == 0 and b >= 8 and g == 0:
                        dve.wait_ge(wst_stored[(b // 4) % 2], 16 * (b // 8))
                    red = dve.tensor_reduce(
                        wst[(b // 4) % 2][:, 4 * g:4 * g + k, BW * (b % 4):BW * (b % 4) + BW],
                        o[:, :, BW:4 * BW].rearrange("p t (a e) -> p t e a", a=3), X_AXIS, ALU.add)
                    red.then_inc(turn_free, 1)

            dve.wait_ge(bounds_ready, 4)
            for b in range(NB):
                lo = dve.value_load(bnd_i[0:1, NB + b:NB + b + 1], min_val=0, max_val=NPAIR - 2)
                hi = dve.value_load(bnd_i[0:1, b:b + 1], min_val=2, max_val=NPAIR)
                with dve.Fori(lo, hi) as pair:
                    for i in range(2):
                        c = pair * 2 + i
                        dve.wait_ge(oh_used, dve.snap(chunks) + 1)
                        dve.tensor_scalar(ohs[0:TP, i, :], iota_s[0:TP, :], srcf[:, bass.ds(c, 1)], None, ALU.is_equal)
                        dve.scalar_tensor_tensor(
                            ohd[0:TP, i, :].rearrange("p (a e) -> p a e", a=4),
                            iota_d[0:TP, BW * b:BW * b + BW].unsqueeze(1).to_broadcast([TP, 4, BW]),
                            dstf[:, bass.ds(c, 1)],
                            parts_flat[:, bass.ds(c * 4, 4)].unsqueeze(2).to_broadcast([TP, 4, BW]),
                            ALU.is_equal, ALU.mult).then_inc(oh_ready, 1)
                        dve.reg_add(chunks, chunks, 1)
                if b >= 1:
                    read_block(b - 1)
            read_block(NB - 1)

        def graph_act(act, n):
            act.dma_start(V[0:TP, 0, 0:NCH].bitcast(I32), A["src"]).then_inc(act_dma, 16)
            act.dma_start(V[0:TP, 1, 0:NCH].bitcast(I32), A["dst"]).then_inc(act_dma, 16)
            act.dma_start(ew, A["ew"]).then_inc(act_dma, 16)
            act.dma_start(cols[:, :], A["cols"]).then_inc(act_dma, 16)
            act.dma_start(wg[:, :], A["wg"]).then_inc(act_dma, 16)
            n.dma += 5
            act.wait_ge(act_dma, 16 * n.dma)
            act.wait_ge(max_ready, 1)
            act.activation(exw, ew, ACT.Exp, bias=smw[0:TP, 2:3]).then_inc(act_out, 1)
            n.a += 1
            for b in range(NB):
                act.wait_ge(blk_full, b + 1)
                if b >= 2:
                    act.wait_ge(turn_full, 3 + 3 * (b - 1))
                act.activation(stg[b % 2].rearrange("p (m e) -> p m e", m=3), ps[:, 3 * (b % 2):3 * (b % 2) + 3, 0:MW],
                               ACT.Copy).then_inc(blk_free, 1)
                if b % 4 == 3 and b >= 7:
                    graph_store(act, n, b // 4 - 1)
            graph_store(act, n, NB // 4 - 1)

        def graph_store(act, n, g):
            act.wait_ge(turn_free, 3 * (4 * g + 4))
            act.dma_start(d_w[:, :, 128 * g:128 * g + 128].rearrange("t p e -> p t e"), wst[g % 2]).then_inc(wst_stored[g % 2], 16)

        def transpose_w_act(act, n):
            for i in range(2):
                act.wait_ge(wst_stored[i], 16 * (NB // 8))
            act.dma_start(d_cnt, AR[0:TP, :]).then_inc(cnt_stored, 16)
            for t in range(NT + 1):
                if t < NT:
                    if t >= 2:
                        act.wait_ge(psum_free, n.free + 3 * (t - 1))
                        act.wait_ge(dve_out, n.d + t - 1)
                    act.dma_start(win[t % 2], d_w[t]).then_inc(win_loaded[t % 2], 16)
                if t >= 1:
                    u = t - 1
                    if u >= 2:
                        act.wait_ge(wt_stored[u % 2], 16 * (u // 2))
                    for g in range(3):
                        j = n.full + 3 * u + g
                        k = min(4, NT - 4 * g)
                        act.wait_ge(psum_full, j + 1)
                        act.activation(wout[u % 2][:, TP * 4 * g:TP * (4 * g + k)], bank(j)[0:TP, 0:TP * k], ACT.Copy)\
                           .then_inc(psum_free, 1)
                    act.wait_ge(psum_free, n.free + 3 * u + 3)
                    act.dma_start(d_wt[:, :, TP * u:TP * u + TP].rearrange("t p e -> p t e"),
                                  wout[u % 2].rearrange("p (t e) -> p t e", t=NT)).then_inc(wt_stored[u % 2], 16)
            n.full += 3 * NT
            n.free += 3 * NT
            n.d += NT
            for i in range(2):
                act.wait_ge(wt_stored[i], 16 * (NT // 2))
            act.wait_ge(cnt_stored, 16)
            act.wait_ge(psum_free, n.free)

        def transpose_w_pe(pe, n):
            for t in range(NT):
                pe.wait_ge(win_loaded[t % 2], 16 * (t // 2 + 1))
                for g in range(3):
                    j = n.full
                    if j >= 8:
                        pe.wait_ge(psum_free, j - 7)
                    for q in range(4 * g, min(4 * g + 4, NT)):
                        last = pe.transpose(bank(j)[0:TP, TP * (q - 4 * g):TP * (q - 4 * g) + TP],
                                            win[t % 2][:, TP * q:TP * q + TP], ident[0:TP, 0:TP])
                    last.then_inc(psum_full, 1)
                    n.full += 1
            n.free += 3 * NT
            n.d += NT

        def transpose_w_dve(dve, n):
            for t in range(NT):
                dve.wait_ge(win_loaded[t % 2], 16 * (t // 2 + 1))
                dve.tensor_reduce(rsum[0:TP, t:t + 1], win[t % 2][:, 0:N], X_AXIS, ALU.add).then_inc(dve_out, 1)
            n.full += 3 * NT
            n.free += 3 * NT
            n.d += NT

        @block.sync
        def _(sp):
            for u in range(len(UNITS)):
                if u >= 1:
                    sp.wait_ge(w_ready, u)
                sp.dma_start(wraw[:, :], A["units"][u]).then_inc(w_loaded, 16)

        @block.gpsimd
        def _(pool):
            made = 0

            def const(ins):
                nonlocal made
                ins.then_inc(consts_ready, 1)
                made += 1
                pool.wait_ge(consts_ready, made)

            const(pool.memset(ident[:, :], 0.0))
            const(pool.memset(ones[:, :], 1.0))
            const(pool.memset(mask_h[:, :, :], 0.0))
            const(pool.memset(mask_p[:, :], 0.0))
            const(pool.memset(epsc, EPS))
            const(pool.memset(lneps, LN_EPS))
            const(pool.affine_select(out=ident[:, :], in_=ident[:, :], compare_op=ALU.not_equal, fill=1.0,
                                     base=0, pattern=[[-1, 128]], channel_multiplier=1))
            for h in range(2):
                for c in range(KC):
                    const(pool.memset(mask_h[64 * h:64 * h + 64, c, 2 * c + h:2 * c + h + 1], 1.0))
                const(pool.memset(mask_p[64 * h:64 * h + 64, 64 * h:64 * h + 64], 1.0))
            const(pool.iota(iota8[:, :], [[-1, 8]], base=8, channel_multiplier=0,
                            allow_small_or_imprecise_dtypes=True))
            const(pool.iota(iota_s, [[1, 3 * MW]], base=0, channel_multiplier=0))
            const(pool.iota(iota_d, [[1, NPAD]], base=0, channel_multiplier=0, allow_small_or_imprecise_dtypes=True))
            const(pool.iota(iota_b, [[BW, NB]], base=0, channel_multiplier=0, allow_small_or_imprecise_dtypes=True))
            const(pool.iota(iota_c[:, 0:1], [[1, 1]], base=1, channel_multiplier=1,
                            allow_small_or_imprecise_dtypes=True))
            const(pool.iota(iota_c[:, 1:2], [[1, 1]], base=NPAIR, channel_multiplier=-1,
                            allow_small_or_imprecise_dtypes=True))
            assert made == CONSTS
            pool.wait_ge(dve_seq, 4)
            pool.partition_all_reduce(smw[0:TP, 1:2], smw[0:TP, 0:1], TP, bass.bass_isa.ReduceOp.max)\
                .then_inc(pool_max, 1)
            pool.wait_ge(pool_max, 1)
            pool.tensor_scalar(smw[0:TP, 2:3], smw[0:TP, 1:2], 0.0, -1.0, ALU.max, ALU.mult).then_inc(max_ready, 1)
            for u in range(len(UNITS)):
                pool.wait_ge(w_loaded, 16 * (u + 1))
                if u >= 2:
                    pool.wait_ge(w_used, u - 1)
                pool.tensor_copy(wH[:, u % 2, :], wraw[:, :]).then_inc(pool_seq, 1)
                pool.wait_ge(pool_seq, u + 1)
                pool.tensor_tensor(wL[:, u % 2, :], wraw[:, :], wH[:, u % 2, :].bitcast(F32),
                                   ALU.subtract).then_inc(w_ready, 1)

        @block.tensor
        def _(pe):
            n = Counts()

            def job(mms):
                j = n.full
                if j >= 8:
                    pe.wait_ge(psum_free, j - 7)
                last = None
                for i, (o, l, r) in enumerate(mms):
                    last = pe.matmul(o, lhsT=l, rhs=r, start=(i == 0), stop=(i == len(mms) - 1),
                                     skip_group_check=True)
                last.then_inc(psum_full, 1)
                n.full += 1

            def unit():
                u = n.unit
                pe.wait_ge(w_ready, u + 1)
                return wH[:, u % 2, :], wL[:, u % 2, :]

            def unit_done():
                n.unit += 1
                pe.drain().then_inc(w_used, 1)

            def gemm_cols(XHs, XLs, K, WHv, WLv, M, ready=None):
                for (c0, w) in CH:
                    for m in range(M):
                        o = bank(n.full)[:, 0:w]
                        mms = []
                        for k in range(K):
                            a, b = WHv[:, k, 128 * m:128 * m + 128], WLv[:, k, 128 * m:128 * m + 128]
                            mms += [(o, a, XHs[:, k, c0:c0 + w]), (o, b, XHs[:, k, c0:c0 + w]),
                                    (o, a, XLs[:, k, c0:c0 + w])]
                        job(mms)

            def gemm_rows(XHs, XLs, K, WHv, WLv, NW, ready=None):
                for t in range(NT):
                    if ready:
                        ready(t)
                    o = bank(n.full)[0:TP, 0:NW]
                    s = slice(TP * t, TP * t + TP)
                    mms = []
                    for k in range(K):
                        mms += [(o, XHs[:, k, s], WHv[:, k, 0:NW]), (o, XHs[:, k, s], WLv[:, k, 0:NW]),
                                (o, XLs[:, k, s], WHv[:, k, 0:NW])]
                    job(mms)

            def v4(w):
                return w.rearrange("p (k n) -> p k n", k=KC)

            def turn(src, K=KC):
                for t in range(NT):
                    j = n.full
                    if j >= 8:
                        pe.wait_ge(psum_free, j - 7)
                    for k in range(K):
                        last = pe.transpose(bank(j)[:, TP * k:TP * k + TP], src(t)[:, 128 * k:128 * k + 128],
                                            ident[0:TP, 0:TP])
                    last.then_inc(psum_full, 1)
                    n.full += 1

            def turn_back(srcT):
                for t in range(NT):
                    j = n.full
                    if j >= 8:
                        pe.wait_ge(psum_free, j - 7)
                    for k in range(KC):
                        last = pe.transpose(bank(j)[0:TP, 128 * k:128 * k + 128],
                                            srcT[:, k, TP * t:TP * t + TP], ident[:, :])
                    last.then_inc(psum_full, 1)
                    n.full += 1

            def end():
                end_stage(pe, n)

            def normed(k=1):
                n.d += k

            def x_to_cols(src):
                turn(src)
                end()

            pe.wait_ge(consts_ready, CONSTS)
            graph_pe(pe, n)
            end()
            transpose_w_pe(pe, n)
            end()
            normed()
            end()
            x_to_cols(lambda t: R1t[:, t, :])
            H_, L_ = unit()
            gemm_cols(XH, XL, KC, v4(H_), v4(L_), KC)
            unit_done()
            for _ in range(2):
                H_, L_ = unit()
                gemm_rows(XH, XL, KC, v4(H_), v4(L_), D)
                unit_done()
            normed(12 + NT)
            end()
            j = n.full
            pe.wait_ge(psum_free, j - 6)
            for c in range(KC):
                for t in range(NT):
                    pe.matmul(bank(j)[:, 128 * c:128 * c + 128], lhsT=A2t[:, t, 128 * c:128 * c + 128],
                              rhs=R2t[:, t, 128 * c:128 * c + 128], start=t == 0, stop=t == NT - 1,
                              skip_group_check=True)
            for c in range(KC):
                for t in range(NT):
                    last = pe.matmul(bank(j + 1)[:, 2 * c:2 * c + 2], lhsT=A2t[:, t, 128 * c:128 * c + 128],
                                     rhs=ones[0:TP, 0:2], start=t == 0, stop=t == NT - 1,
                                     skip_group_check=True)
            last.then_inc(psum_full, 1)
            n.full += 1
            end()
            heads_dot(pe, n, A1c, blkA, None)
            rows_attn(pe, n, A1c)
            end()
            x_to_cols(lambda t: A2t[:, t, :])
            H_, L_ = unit()
            gemm_rows(XH, XL, KC, v4(H_), v4(L_), D)
            unit_done()
            end()
            normed()
            end()
            x_to_cols(lambda t: R2t[:, t, :])
            d0 = n.d
            H_, L_ = unit()
            gemm_cols(XH, XL, KC, H_[:, 0:1024].rearrange("p (k n) -> p k n", k=KC),
                      L_[:, 0:1024].rearrange("p (k n) -> p k n", k=KC), 2)
            hidden_ready = lambda t: pe.wait_ge(dve_out, d0 + 2 * (1 + min(t // 4, 2)))
            gemm_rows(HH, HL, 2, H_[:, 1024:2048].rearrange("p (k n) -> p k n", k=2),
                      L_[:, 1024:2048].rearrange("p (k n) -> p k n", k=2), D, hidden_ready)
            unit_done()
            n.d += 6
            end()
            normed(2)
            end()
            turn(lambda t: R1t[:, t, :])
            for (c0, w) in CH:
                job([(bank(n.full)[:, 0:w], ones[0:TP, :], CT[:, t, c0:c0 + w]) for t in range(NT)])
            end()
            for l in range(3):
                for _ in range(2):
                    H_, L_ = unit()
                    gemm_rows(XH, XL, KC, v4(H_), v4(L_), D)
                    unit_done()
                end()
                for (c0, w) in CH:
                    for m in range(KC):
                        job([(bank(n.full)[:, 0:w], R2t[:, t, 128 * m:128 * m + 128], CT[:, t, c0:c0 + w])
                             for t in range(NT)])
                end()
                H_, L_ = unit()
                gemm_rows(XH, XL, KC, v4(H_), v4(L_), D)
                unit_done()
                end()
                if l < 2:
                    normed()
                    end()
                    x_to_cols(lambda t: R1t[:, t, :])
            end()
            normed()
            end()
            x_to_cols(lambda t: R1t[:, t, :])
            gate_logits(pe, n, 0, 8)
            normed()
            end()
            for i in range(2):
                for (c0, w) in CH:
                    j = n.full
                    pe.wait_ge(psum_free, j - 7)
                    for t in range(c0 // TP, (c0 + w) // TP):
                        last = pe.matmul(bank(j)[:, TP * t - c0:TP * t - c0 + TP],
                                         lhsT=wtop[0:TP, NT * i + t:NT * i + t + 1].to_broadcast([TP, 128]),
                                         rhs=ident[0:TP, 0:TP], start=True, stop=True, skip_group_check=True)
                    last.then_inc(psum_full, 1)
                    n.full += 1
            pe.wait_ge(psum_free, n.full - 7)
            pe.matmul(bank(n.full)[:, :], lhsT=lgs2[0:E0, :], rhs=b2f[0:E0, :], start=True, stop=True,
                      skip_group_check=True).then_inc(psum_full, 1)
            n.full += 1
            end()

            def expert(steps=1):
                d0 = n.d
                H_, L_ = unit()
                gemm_cols(XH, XL, KC, H_[:, 0:1024].rearrange("p (k n) -> p k n", k=KC),
                          L_[:, 0:1024].rearrange("p (k n) -> p k n", k=KC), 2)
                hidden_ready = lambda t: pe.wait_ge(dve_out, d0 + 2 * steps * (1 + min(t // 4, 2)))
                gemm_rows(HH, HL, 2, H_[:, 1024:2048].rearrange("p (k n) -> p k n", k=2),
                          L_[:, 1024:2048].rearrange("p (k n) -> p k n", k=2), D, hidden_ready)
                unit_done()
                n.d += 6 * steps

            for e in range(E0):
                expert(2)
            end()
            normed()
            end()
            x_to_cols(lambda t: R1t[:, t, :])
            for _ in range(2):
                H_, L_ = unit()
                gemm_cols(XH, XL, KC, v4(H_), v4(L_), KC)
                unit_done()
            end()
            heads_dot(pe, n, A1c, blkA, 1)
            heads_dot(pe, n, A2c, blkB, 1)
            end()
            turn_back(A1c)
            end()
            weighted_sums(pe, n, 0)
            end()
            turn_back(A2c)
            end()
            weighted_sums(pe, n, 1)
            end()
            heads_dot(pe, n, A1c, blkA, 1)
            heads_dot(pe, n, A2c, blkB, 1)
            normed(2)
            end()
            job([(bank(n.full)[:, 0:80], ones[0:TP, :], s80[4][0:TP, :])])
            end()
            H_, L_ = unit()
            gemm_rows(XH, XL, KC, v4(H_), v4(L_), D)
            unit_done()
            H_, L_ = unit()
            gemm_rows(XH, XL, KC, H_[:, 0:1024].rearrange("p (k n) -> p k n", k=KC),
                      L_[:, 0:1024].rearrange("p (k n) -> p k n", k=KC), 256)
            unit_done()
            end()
            j = n.full
            pe.wait_ge(psum_free, j - 7)
            for c in range(KC):
                for t in range(NT):
                    last = pe.matmul(bank(j)[:, 128 * c:128 * c + 128], lhsT=R1t[:, t, 128 * c:128 * c + 128],
                                     rhs=A2t[:, t, 128 * c:128 * c + 128], start=t == 0, stop=t == NT - 1,
                                     skip_group_check=True)
            last.then_inc(psum_full, 1)
            n.full += 1
            end()
            rows_attn(pe, n, A1c)
            end()
            x_to_cols(lambda t: R1t[:, t, :])
            H_, L_ = unit()
            gemm_rows(XH, XL, KC, v4(H_), v4(L_), D)
            unit_done()
            end()
            for (c0, w) in CH:
                j = n.full
                pe.wait_ge(psum_free, j - 7)
                for t in range(c0 // TP, (c0 + w) // TP):
                    last = pe.matmul(bank(j)[:, TP * t - c0:TP * t - c0 + TP],
                                     lhsT=rinv[0:TP, t:t + 1].to_broadcast([TP, 128]),
                                     rhs=ident[0:TP, 0:TP], start=True, stop=True, skip_group_check=True)
                last.then_inc(psum_full, 1)
                n.full += 1
            end()
            for half in range(2):
                for i, (c0, w) in enumerate(CH):
                    s = (3 * half + i) % 2
                    pe.wait_ge(slab_loaded[s], 16 * ((3 * half + i) // 2 + 1))
                    for m in range(2):
                        slab = slab_of(s)
                        src = MfA if half == 0 else MfB
                        job([(bank(n.full)[:, 0:w], src[:, t, 128 * m:128 * m + 128], slab[:, t, 0:w])
                             for t in range(NT)])
            end()
            H_, L_ = unit()
            gemm_rows(XH, XL, KC, H_[:, 1024:1536].rearrange("p (k n) -> p k n", k=KC),
                      L_[:, 1024:1536].rearrange("p (k n) -> p k n", k=KC), 128)
            end()
            normed()
            end()
            turn(lambda t: hg[:, t, :], 1)
            end()
            gemm_rows(HH, HL, 1, H_[:, 1536:2048].rearrange("p (k n) -> p k n", k=1),
                      L_[:, 1536:2048].rearrange("p (k n) -> p k n", k=1), D)
            unit_done()
            end()
            normed()
            end()
            x_to_cols(lambda t: R1t[:, t, :])
            gate_logits(pe, n, 8, 16)
            normed()
            end()
            for t in range(NT):
                j = n.full
                pe.wait_ge(psum_free, j - 7)
                pe.transpose(bank(j)[0:E1, 0:TP], pr[0:TP, E1 * t:E1 * t + E1], ident[0:TP, 0:TP]).then_inc(psum_full, 1)
                n.full += 1
            end()
            for t in range(NT):
                job([(bank(n.full)[0:TP, :], mT[:, TP * t:TP * t + TP], b2f[0:E1, :])])
            for e in range(1 + E1):
                expert()

        @block.scalar
        def _(act):
            n = Counts()

            def end():
                if n.rows:
                    act.wait_ge(rows_loaded, 16 * n.rows)
                end_stage(act, n)

            def load_rows(*names):
                for name in names:
                    act.dma_start(rows[:, ROW_SLOT[name], :],
                                  A["rows"][ROWS.index(name):ROWS.index(name) + 1, :].to_broadcast([128, D]))\
                       .then_inc(rows_loaded, 16)
                    n.rows += 1

            def loaded():
                n.dma += 1

            def copies(k, dst, func=ACT.Copy):
                for i in range(k):
                    j = n.full + i
                    act.wait_ge(psum_full, j + 1)
                    o, src = dst(i, bank(j))
                    act.activation(o, src, func).then_inc(psum_free, 1)
                n.full += k
                n.free += k

            def split_cols(K=KC, XHd=None):
                XHd = XH if XHd is None else XHd
                for t in range(NT):
                    act.wait_ge(psum_full, n.full + t + 1)
                    act.activation(XHd[:, 0:K, TP * t:TP * t + TP],
                                   bank(n.full + t)[:, 0:TP * K].rearrange("p (k e) -> p k e", k=K), ACT.Copy)\
                       .then_inc(act_out, 1)
                n.full += NT
                n.free += NT
                n.a += NT

            def norm():
                act.wait_ge(dve_out, n.d + 1)
                act.activation(std[0:TP, :], mv[0:TP, :].rearrange("p (t two) -> p t two", two=2)[:, :, 1],
                               ACT.Sqrt, bias=lneps[0:TP, :]).then_inc(act_out, 1)
                n.d += 1
                n.a += 1

            def skip(full, a=0, d=0):
                n.full += full
                n.free += full
                n.a += a
                n.d += d

            def relu_hidden():
                i = 0
                for (c0, w) in CH:
                    for m in range(2):
                        act.wait_ge(psum_free, n.free + i + 1)
                        act.activation(HH[:, m, c0:c0 + w], V[:, i % 4, 0:w], ACT.Copy).then_inc(act_out, 1)
                        i += 1
                skip(6, 6, 6)
                skip(NT)

            act.wait_ge(consts_ready, CONSTS)
            graph_act(act, n)
            end()
            transpose_w_act(act, n)
            act.wait_ge(dve_out, n.d)
            act.dma_start(R1t, A["x"].rearrange("(t p) d -> p t d", p=TP)).then_inc(in_loaded, 16)
            load_rows("bk", "bv", "bo", "mg1", "mbe1")
            end()
            act.activation(wgH[:, :, :], wg[:, :].rearrange("p (k e) -> p k e", k=KC), ACT.Copy).then_inc(act_out, 1)
            n.a += 1
            norm()
            end()
            split_cols()
            end()
            i = 0
            for (c0, w) in CH:
                for m in range(KC):
                    act.wait_ge(dve_out, n.d + i + 1)
                    act.activation(V[:, i % 4, 0:w], V[:, i % 4, 0:w], ACT.Exp).then_inc(act_out, 1)
                    i += 1
            skip(12, 12, 12)
            for t in range(NT):
                act.wait_ge(dve_out, n.d + t + 1)
                act.activation(V[0:TP, t % 4, :], V[0:TP, t % 4, :], ACT.Exp).then_inc(act_out, 1)
            skip(NT, NT, NT)
            skip(NT)
            end()
            skip(1)
            load_rows("mb2")
            end()
            skip(1 + NT)
            end()
            split_cols()
            end()
            skip(NT)
            end()
            norm()
            end()
            split_cols()
            end()
            relu_hidden()
            load_rows("mg2", "mbe2", "bp0", "bl0")
            end()
            act.dma_start(A1t, A["x"].rearrange("(t p) d -> p t d", p=TP)).then_inc(in_loaded, 16)
            norm()
            act.wait_ge(dve_out, n.d + 1)
            n.d += 1
            act.dma_start(d_acc, R2t).then_inc(act_dma, 16)
            act.dma_start(AR[0:TP, :], d_cnt).then_inc(act_dma, 16)
            n.dma += 2
            act.wait_ge(act_dma, 16 * n.dma)
            end()
            split_cols()
            skip(3)
            end()
            for l in range(3):
                for t in range(NT):
                    act.wait_ge(psum_free, n.free + t + 1)
                    act.activation(R2t[:, t, :], R2t[:, t, :], ACT.Relu).then_inc(act_out, 1)
                skip(NT, NT)
                skip(NT)
                if l < 2:
                    load_rows(f"g{l}", f"be{l}", f"bp{l + 1}")
                end()
                i = 0
                for (c0, w) in CH:
                    for m in range(KC):
                        act.wait_ge(psum_free, n.free + i + 1)
                        act.activation(XH[:, m, c0:c0 + w], V[:, i % 4, 0:w], ACT.Copy).then_inc(act_out, 1)
                        i += 1
                skip(12, 12)
                if l < 2:
                    load_rows(f"bl{l + 1}")
                if l == 2:
                    act.dma_start(R2t, d_acc).then_inc(act_dma, 16)
                    n.dma += 1
                end()
                skip(NT)
                end()
                if l < 2:
                    norm()
                    end()
                    split_cols()
                    end()
            end()
            norm()
            end()
            split_cols()
            act.dma_start(b2f[0:E0, :], A["b2f"]).then_inc(act_dma, 16)
            n.dma += 1
            end()
            act.wait_ge(dve_out, n.d + 1)
            act.activation(pr[0:TP, 0:80], lg[0:TP, 0:80], ACT.Exp).then_inc(act_out, 1)
            act.wait_ge(act_dma, 16 * n.dma)
            skip(1, 1, 1)
            end()
            copies(6, lambda i, b: (BC[:, i // 3, CH[i % 3][0]:CH[i % 3][0] + CH[i % 3][1]], b[:, 0:CH[i % 3][1]]))
            skip(1)
            end()
            for e in range(E0):
                i = 0
                for (c0, w) in CH:
                    for m in range(2):
                        bias = cols[:, COLS["fb1"] + 2 * e + m:COLS["fb1"] + 2 * e + m + 1]
                        act.wait_ge(psum_free, n.free + i + 1)
                        for s in range(2):
                            v = V[:, 2 * (i % 2) + s, 0:w]
                            act.activation(v, v, ACT.Gelu, bias=bias).then_inc(act_out, 1)
                        act.wait_ge(dve_out, n.d + 2 * i + 1)
                        act.activation(HH[:, m, c0:c0 + w], V[:, 2 * (i % 2), 0:w], ACT.Copy).then_inc(act_out, 1)
                        i += 1
                skip(6, 18, 12)
                skip(NT)
            end()
            norm()
            load_rows("gnnA", "gnnB", "gnnb2", "bproj")
            end()
            split_cols()
            end()
            for (dst, sums) in ((A1c, acc12), (A2c, acc12b)):
                i = 0
                for (c0, w) in CH:
                    for m in range(KC):
                        act.wait_ge(psum_full, n.full + i + 1)
                        act.activation(dst[:, m, c0:c0 + w], bank(n.full + i)[:, 0:w], ACT.Sigmoid,
                                       accum_out=sums[:, 4 * (i // 4) + m:4 * (i // 4) + m + 1]).then_inc(psum_free, 1)
                        i += 1
                skip(12)
            act.wait_ge(psum_free, n.free)
            end()
            skip(2)
            end()
            copies(NT, lambda t, b: (R1t[:, t, :], b[0:TP, :]))
            end()
            skip(1)
            end()
            copies(NT, lambda t, b: (R1t[:, t, :], b[0:TP, :]))
            end()
            skip(1)
            end()
            act.wait_ge(dve_out, n.d + 1)
            act.activation(s80[2][0:TP, :], s80[2][0:TP, :], ACT.Sigmoid).then_inc(act_out, 1)
            act.wait_ge(dve_out, n.d + 2)
            act.activation(s80[4][0:TP, :], s80[4][0:TP, :], ACT.Exp).then_inc(act_out, 1)
            skip(2, 2, 2)
            end()
            skip(1)
            end()
            skip(2 * NT)
            end()
            skip(1)
            end()
            skip(NT)
            end()
            split_cols()
            end()
            skip(NT)
            end()
            copies(3, lambda i, b: (BC[:, 0, CH[i][0]:CH[i][0] + CH[i][1]], b[:, 0:CH[i][1]]))
            end()
            def load_slab(i):
                half, (c0, w) = i // 3, CH[i % 3]
                act.dma_start(slab_of(i % 2)[:, :, 0:w],
                              (d_wt if half == 0 else d_w)[:, :, c0:c0 + w].rearrange("t p e -> p t e"))\
                   .then_inc(slab_loaded[i % 2], 16)
            load_slab(0)
            load_slab(1)
            for i in range(6):
                half, (c0, w) = i // 3, CH[i % 3]
                for m in range(2):
                    q = 2 * i + m
                    if half == 0:
                        act.wait_ge(psum_free, n.free + q + 1)
                        src = V[:, q % 4, 0:w]
                    else:
                        act.wait_ge(psum_full, n.full + q + 1)
                        src = bank(n.full + q)[:, 0:w]
                    act.activation(XH[:, 2 * half + m, c0:c0 + w], src, ACT.Copy).then_inc(act_out, 1)
                if i < 4:
                    act.wait_ge(psum_full, n.full + 2 * i + 2)
                    load_slab(i + 2)
            skip(12, 12)
            end()
            skip(NT)
            end()
            norm()
            end()
            split_cols(1, HH)
            end()
            skip(NT)
            load_rows("bs2")
            end()
            norm()
            end()
            split_cols()
            end()
            act.dma_start(b2f[0:E1, :], A["b2e"]).then_inc(act_dma, 16)
            n.dma += 1
            act.wait_ge(dve_out, n.d + 1)
            act.activation(pr[0:TP, :], lg[0:TP, :], ACT.Exp).then_inc(act_out, 1)
            act.wait_ge(act_dma, 16 * n.dma)
            skip(1, 1, 1)
            end()
            copies(NT, lambda t, b: (mT[:, TP * t:TP * t + TP], b[0:E1, 0:TP]))
            end()
            skip(NT)
            for e in range(1 + E1):
                base = COLS["bs1"] if e == 0 else COLS["eb1"] + 2 * (e - 1)
                i = 0
                for (c0, w) in CH:
                    for m in range(2):
                        act.wait_ge(psum_full, n.full + i + 1)
                        if i >= 4:
                            act.wait_ge(dve_out, n.d + i - 3)
                        act.wait_ge(psum_free, n.free + i)
                        act.activation(V[:, i % 4, 0:w], bank(n.full + i)[:, 0:w], ACT.Gelu,
                                       bias=cols[:, base + m:base + m + 1]).then_inc(psum_free, 1)
                        act.wait_ge(psum_free, n.free + i + 1)
                        act.activation(HH[:, m, c0:c0 + w], V[:, i % 4, 0:w], ACT.Copy).then_inc(act_out, 1)
                        i += 1
                skip(6, 6, 6)
                skip(NT)
            act.wait_ge(psum_free, n.free)
            act.dma_start(out.rearrange("(t p) d -> p t d", p=TP), R2t).then_inc(out_stored, 16)
            act.wait_ge(out_stored, 16)

        @block.vector
        def _(dve):
            n = Counts()

            def end():
                end_stage(dve, n)

            def own(ins):
                ins.then_inc(dve_seq, 1)
                n.seq += 1

            def settle():
                dve.wait_ge(dve_seq, n.seq)

            def skip(full, a=0, d=0):
                n.full += full
                n.free += full
                n.a += a
                n.d += d

            def split_cols(K=KC, Hd=None, Ld=None):
                Hd, Ld = (XH, XL) if Hd is None else (Hd, Ld)
                for t in range(NT):
                    s = slice(TP * t, TP * t + TP)
                    dve.wait_ge(act_out, n.a + t + 1)
                    dve.tensor_tensor(Ld[:, 0:K, s],
                                      bank(n.full + t)[:, 0:TP * K].rearrange("p (k e) -> p k e", k=K),
                                      Hd[:, 0:K, s].bitcast(F32), ALU.subtract).then_inc(psum_free, 1)
                skip(NT, NT)

            def norm(src, dst, w=D, g=None, b=None):
                for t in range(NT):
                    own(dve.bn_stats(bnst[0:TP, 6 * t:6 * t + 6], src[:, t, :]))
                settle()
                for t in range(NT):
                    ins = dve.bn_aggr(mv[0:TP, 2 * t:2 * t + 2], bnst[0:TP, 6 * t:6 * t + 6])
                    if t < NT - 1:
                        own(ins)
                    else:
                        ins.then_inc(dve_out, 1)
                m2 = mv[0:TP, :].rearrange("p (t two) -> p t two", two=2)
                dve.wait_ge(dve_out, n.d + 1)
                settle()
                own(dve.tensor_scalar(u10[0:TP, :], m2[:, :, 1], LN_EPS, None, ALU.add))
                dve.wait_ge(act_out, n.a + 1)
                own(dve.reciprocal(rstd[0:TP, :], std[0:TP, :]))
                settle()
                own(dve.tensor_tensor(t10[0:TP, :], rstd[0:TP, :], rstd[0:TP, :], ALU.mult))
                settle()
                own(dve.tensor_tensor(t10[0:TP, :], t10[0:TP, :], u10[0:TP, :], ALU.mult))
                settle()
                own(dve.tensor_scalar(t10[0:TP, :], t10[0:TP, :], -0.5, 1.5, ALU.mult, ALU.add))
                settle()
                own(dve.tensor_tensor(rstd[0:TP, :], rstd[0:TP, :], t10[0:TP, :], ALU.mult))
                settle()
                for t in range(NT):
                    own(dve.tensor_scalar(dst[:, t, :], src[:, t, :], m2[:, t, 0:1], rstd[0:TP, t:t + 1],
                                          ALU.subtract, ALU.mult))
                if g is not None:
                    settle()
                    own(dve.tensor_tensor(dst, dst, g.unsqueeze(1).to_broadcast([TP, NT, w]), ALU.mult))
                    settle()
                    own(dve.tensor_tensor(dst, dst, b.unsqueeze(1).to_broadcast([TP, NT, w]), ALU.add))
                settle()
                n.d += 1
                n.a += 1

            def add_rows(dst, other):
                for t in range(NT):
                    dve.wait_ge(psum_full, n.full + t + 1)
                    dve.tensor_tensor(dst(t), bank(n.full + t)[0:TP, 0:dst(t).shape[1]], other(t), ALU.add)\
                       .then_inc(psum_free, 1)
                skip(NT)

            def per_head(t, s):
                return s[0:TP, 8 * t:8 * t + 8].unsqueeze(2).to_broadcast([TP, HEADS, 64])

            def heads(ap):
                return ap.rearrange("p (h e) -> p h e", h=HEADS)

            def c8(b):
                return b.rearrange("p (c h) -> p c h", c=KC)

            graph_dve(dve, n, None)
            end()
            transpose_w_dve(dve, n)
            dve.wait_ge(dve_out, n.d)
            own(dve.tensor_scalar(t10[0:TP, :], rsum[0:TP, :], EPS, None, ALU.add))
            own(dve.tensor_scalar(valid[0:TP, :], rsum[0:TP, :], 0.0, None, ALU.is_gt))
            settle()
            own(dve.reciprocal(rinv[0:TP, :], t10[0:TP, :]))
            settle()
            end()
            dve.wait_ge(in_loaded, 16)
            dve.wait_ge(act_out, n.a + 1)
            own(dve.tensor_tensor(wgL[:, :, :], wg[:, :].rearrange("p (k e) -> p k e", k=KC), wgH[:, :, :].bitcast(F32),
                                  ALU.subtract))
            n.a += 1
            norm(R1t, R1t)
            end()
            split_cols()
            end()
            def q_tail(i):
                c0, w = CH[i // KC]
                o = A1c[:, i % KC, c0:c0 + w]
                dve.wait_ge(act_out, n.a + i + 1)
                dve.wait_ge(psum_free, n.free + i + 1)
                own(dve.tensor_tensor(o, o, V[:, i % 4, 0:w], ALU.add))

            for i in range(12):
                c0, w = CH[i // KC]
                m = i % KC
                b = cols[:, COLS["bq"] + m:COLS["bq"] + m + 1]
                dve.wait_ge(psum_full, n.full + i + 1)
                dve.tensor_scalar(V[:, i % 4, 0:w], bank(n.full + i)[:, 0:w], b, 0.0, ALU.add, ALU.min)\
                   .then_inc(dve_out, 1)
                dve.tensor_scalar(A1c[:, m, c0:c0 + w], bank(n.full + i)[:, 0:w], b, 0.0, ALU.add, ALU.max)\
                   .then_inc(psum_free, 1)
                if i >= 1:
                    q_tail(i - 1)
            q_tail(11)
            skip(12, 12, 12)
            settle()

            def k_tail(t):
                o = A2t[:, t, :]
                dve.wait_ge(act_out, n.a + t + 1)
                own(dve.scalar_tensor_tensor(o, o, 0.0, V[0:TP, t % 4, :], ALU.max, ALU.add))

            for t in range(NT):
                dve.wait_ge(psum_full, n.full + t + 1)
                dve.tensor_tensor(A2t[:, t, :], bank(n.full + t)[0:TP, :], row("bk"), ALU.add).then_inc(psum_free, 1)
                dve.wait_ge(psum_free, n.free + t + 1)
                dve.tensor_scalar(V[0:TP, t % 4, :], A2t[:, t, :], 0.0, None, ALU.min).then_inc(dve_out, 1)
                if t >= 1:
                    k_tail(t - 1)
            k_tail(NT - 1)
            skip(NT, NT, NT)
            add_rows(lambda t: R2t[:, t, :], lambda t: row("bv"))
            end()
            dve.wait_ge(psum_full, n.full + 1)
            j = n.full
            own(dve.tensor_tensor(kvb, bank(j).rearrange("p (c e) -> p c e", c=KC),
                                  mask_p[:, :].unsqueeze(1).to_broadcast([128, KC, 128]), ALU.mult))
            dve.tensor_tensor(c8(blkA), mask_h[:, :, :],
                              bank(j + 1)[:, 0:8].rearrange("p (c two) -> p c two", two=2)[:, :, 0:1]
                              .to_broadcast([128, KC, HEADS]), ALU.mult).then_inc(psum_free, 1)
            skip(1)
            end()
            dve.wait_ge(psum_full, n.full + 1)
            dve.tensor_scalar(s80[0][0:TP, :], bank(n.full)[0:TP, 0:80], EPS, None, ALU.add).then_inc(psum_free, 1)
            dve.wait_ge(psum_free, n.free + 1)
            own(dve.reciprocal(s80[1][0:TP, :], s80[0][0:TP, :]))
            settle()
            skip(1)
            for t in range(NT):
                dve.wait_ge(psum_full, n.full + t + 1)
                dve.tensor_tensor(heads(A2t[:, t, :]), heads(bank(n.full + t)[0:TP, :]), per_head(t, s80[1]), ALU.mult)\
                   .then_inc(psum_free, 1)
            skip(NT)
            end()
            split_cols()
            end()
            for t in range(NT):
                dve.wait_ge(psum_full, n.full + t + 1)
                dve.tensor_tensor(R2t[:, t, :], bank(n.full + t)[0:TP, :], row("bo"), ALU.add).then_inc(psum_free, 1)
                if t >= 1:
                    dve.wait_ge(psum_free, n.free + t)
                    own(dve.tensor_tensor(R2t[:, t - 1, :], R2t[:, t - 1, :], R1t[:, t - 1, :], ALU.add))
            dve.wait_ge(psum_free, n.free + NT)
            own(dve.tensor_tensor(R2t[:, NT - 1, :], R2t[:, NT - 1, :], R1t[:, NT - 1, :], ALU.add))
            skip(NT)
            settle()
            end()
            norm(R2t, R2t, D, row("mg1"), row("mbe1"))
            end()
            split_cols()
            end()
            def h_tail(i):
                c0, w = CH[i // 2]
                dve.wait_ge(act_out, n.a + i + 1)
                dve.tensor_tensor(HL[:, i % 2, c0:c0 + w], V[:, i % 4, 0:w], HH[:, i % 2, c0:c0 + w].bitcast(F32),
                                  ALU.subtract).then_inc(dve_out, 1)

            for i in range(6):
                c0, w = CH[i // 2]
                dve.wait_ge(psum_full, n.full + i + 1)
                b = cols[:, COLS["mb1"] + i % 2:COLS["mb1"] + i % 2 + 1]
                dve.tensor_scalar(V[:, i % 4, 0:w], bank(n.full + i)[:, 0:w], b, 0.0, ALU.add, ALU.max)\
                   .then_inc(psum_free, 1)
                if i >= 1:
                    h_tail(i - 1)
            h_tail(5)
            skip(6, 6, 6)
            own(dve.tensor_tensor(R2t, R2t, row("mb2").unsqueeze(1).to_broadcast([TP, NT, D]), ALU.add))
            settle()
            add_rows(lambda t: R2t[:, t, :], lambda t: R2t[:, t, :])
            dve.wait_ge(psum_free, n.free)
            end()
            norm(R2t, R2t, D, row("mg2"), row("mbe2"))
            dve.wait_ge(in_loaded, 32)
            dve.tensor_tensor(R2t, R2t, A1t, ALU.add).then_inc(dve_out, 1)
            n.d += 1
            end()
            split_cols()
            for i, (c0, w) in enumerate(CH):
                dve.wait_ge(psum_full, n.full + i + 1)
                dve.tensor_scalar(V[:, i, 0:w], bank(n.full + i)[:, 0:w], 1.0, None, ALU.max).then_inc(psum_free, 1)
                dve.wait_ge(psum_free, n.free + i + 1)
                own(dve.reciprocal(BC[:, 0, c0:c0 + w], V[:, i, 0:w]))
            skip(3)
            settle()
            end()
            for l in range(3):
                add_rows(lambda t: R2t[:, t, :], lambda t: row(f"bp{l}"))
                skip(0, NT)
                add_rows(lambda t: R1t[:, t, :], lambda t: row(f"bl{l}"))
                end()
                def agg_tail(i):
                    c0, w = CH[i // KC]
                    dve.wait_ge(act_out, n.a + i + 1)
                    own(dve.tensor_tensor(XL[:, i % KC, c0:c0 + w], V[:, i % 4, 0:w],
                                          XH[:, i % KC, c0:c0 + w].bitcast(F32), ALU.subtract))

                for i in range(12):
                    c0, w = CH[i // KC]
                    dve.wait_ge(psum_full, n.full + i + 1)
                    dve.tensor_tensor(V[:, i % 4, 0:w], bank(n.full + i)[:, 0:w], BC[:, 0, c0:c0 + w], ALU.mult)\
                       .then_inc(psum_free, 1)
                    if i >= 1:
                        agg_tail(i - 1)
                agg_tail(11)
                skip(12, 12)
                end()
                add_rows(lambda t: R1t[:, t, :], lambda t: R1t[:, t, :])
                dve.wait_ge(psum_free, n.free)
                if l < 2:
                    own(dve.tensor_scalar(R1t, R1t, 0.0, None, ALU.max))
                    settle()
                end()
                if l < 2:
                    norm(R1t, R1t, D, row(f"g{l}"), row(f"be{l}"))
                    end()
                    split_cols()
                    end()
            dve.wait_ge(act_dma, 16 * 8)
            own(dve.tensor_tensor(R2t, R2t, R1t, ALU.add))
            settle()
            end()
            norm(R2t, R1t)
            end()
            split_cols()
            end()

            def softmax(w, groups):
                G = NT * groups
                l3 = lg[0:TP, 0:8 * G].rearrange("p (g e) -> p g e", e=8)
                p3 = pr[0:TP, 0:8 * G].rearrange("p (g e) -> p g e", e=8)
                own(dve.tensor_reduce(gate[0:TP, 0:G], l3, X_AXIS, ALU.max))
                settle()
                dve.tensor_tensor(l3, l3, gate[0:TP, 0:G].unsqueeze(2).to_broadcast([TP, G, 8]), ALU.subtract)\
                   .then_inc(dve_out, 1)
                dve.wait_ge(act_out, n.a + 1)
                own(dve.tensor_reduce(gate[0:TP, 0:G], p3, X_AXIS, ALU.add))
                settle()
                own(dve.reciprocal(gate[0:TP, 0:G], gate[0:TP, 0:G]))
                settle()
                own(dve.tensor_tensor(p3, p3, gate[0:TP, 0:G].unsqueeze(2).to_broadcast([TP, G, 8]), ALU.mult))
                settle()
                skip(0, 1, 1)
                return p3

            dve.wait_ge(psum_full, n.full + 1)
            dve.tensor_copy(lg[0:TP, 0:80], bank(n.full)[0:TP, 0:80]).then_inc(psum_free, 1)
            dve.wait_ge(psum_free, n.free + 1)
            skip(1)
            p3 = softmax(80, 1)
            for t in range(NT):
                own(dve.max(mtop[0:TP, 8 * t:8 * t + 8], p3[:, t, :]))
            settle()
            m3 = mtop[0:TP, :].rearrange("p (t e) -> p t e", e=8)
            own(dve.tensor_tensor(t10[0:TP, :], m3[:, :, 0], m3[:, :, 1], ALU.add))
            settle()
            own(dve.reciprocal(t10[0:TP, :], t10[0:TP, :]))
            settle()
            for i in range(2):
                own(dve.tensor_tensor(wtop[0:TP, NT * i:NT * i + NT], m3[:, :, i], t10[0:TP, :], ALU.mult))
            own(dve.memset(lgs2[0:E0, :], 2.0))
            settle()
            end()
            skip(6)
            dve.wait_ge(psum_full, n.full + 1)
            dve.tensor_copy(V[0:TP, 0, :], bank(n.full)[0:TP, :]).then_inc(psum_free, 1)
            dve.wait_ge(psum_free, n.free + 1)
            own(dve.tensor_tensor(R2t, R2t, V[0:TP, 0, :].unsqueeze(1).to_broadcast([TP, NT, D]), ALU.add))
            settle()
            skip(1)
            end()
            for e in range(E0):
                def g_tail(i):
                    c0, w = CH[i // 2]
                    v0, v1 = V[:, 2 * (i % 2), 0:w], V[:, 2 * (i % 2) + 1, 0:w]
                    dve.wait_ge(act_out, n.a + 3 * i + 2)
                    dve.tensor_tensor(v0, v0, v1, ALU.add).then_inc(dve_out, 1)
                    dve.wait_ge(act_out, n.a + 3 * i + 3)
                    dve.tensor_tensor(HL[:, i % 2, c0:c0 + w], v0, HH[:, i % 2, c0:c0 + w].bitcast(F32), ALU.subtract)\
                       .then_inc(dve_out, 1)

                for i in range(6):
                    c0, w = CH[i // 2]
                    dve.wait_ge(dve_out, n.d + 2 * (i - 1))
                    dve.wait_ge(psum_full, n.full + i + 1)
                    own(dve.tensor_tensor(V[:, 2 * (i % 2), 0:w], bank(n.full + i)[:, 0:w], BC[:, 0, c0:c0 + w], ALU.mult))
                    dve.tensor_tensor(V[:, 2 * (i % 2) + 1, 0:w], bank(n.full + i)[:, 0:w], BC[:, 1, c0:c0 + w], ALU.mult)\
                       .then_inc(psum_free, 1)
                    if i >= 1:
                        g_tail(i - 1)
                g_tail(5)
                skip(6, 18, 12)
                add_rows(lambda t: R2t[:, t, :], lambda t: R2t[:, t, :])
            dve.wait_ge(psum_free, n.free)
            end()
            norm(R2t, R1t)
            end()
            split_cols()
            end()
            skip(24)
            dve.wait_ge(psum_free, n.free)
            for (sums, col, blk) in ((acc12, qsc, blkB), (acc12b, ksc, blkA)):
                own(dve.tensor_tensor(col, sums[:, 0:4], sums[:, 4:8], ALU.add))
                settle()
                own(dve.tensor_tensor(col, col, sums[:, 8:12], ALU.add))
                settle()
                own(dve.scalar_tensor_tensor(c8(blk), col.unsqueeze(2).to_broadcast([128, KC, HEADS]), EPS,
                                             mask_h[:, :, :], ALU.add, ALU.mult))
                settle()
            end()
            for i in range(2):
                dve.wait_ge(psum_full, n.full + 1)
                dve.tensor_scalar(s80[2 + i][0:TP, :], bank(n.full)[0:TP, 0:80], EPS, None, ALU.add)\
                   .then_inc(psum_free, 1)
                skip(1)
                dve.wait_ge(psum_free, n.free)
                own(dve.reciprocal(s80[i][0:TP, :], s80[2 + i][0:TP, :]))
            settle()
            end()
            skip(NT)
            end()
            for (i, blk) in ((0, blkB), (1, blkA)):
                dve.wait_ge(psum_full, n.full + 1)
                dve.scalar_tensor_tensor(c8(blk), bank(n.full)[:, 0:32].rearrange("p (c h) -> p c h", c=KC), EPS,
                                         mask_h[:, :, :], ALU.add, ALU.mult).then_inc(psum_free, 1)
                skip(1)
                dve.wait_ge(psum_free, n.free)
                end()
                if i == 0:
                    skip(NT)
                    end()
            dve.wait_ge(psum_full, n.full + 1)
            dve.tensor_scalar(s80[2][0:TP, :], bank(n.full)[0:TP, 0:80], EPS, None, ALU.add).then_inc(dve_out, 1)
            dve.sem_inc(psum_free, 1)
            dve.wait_ge(psum_full, n.full + 2)
            dve.tensor_scalar(s80[4][0:TP, :], bank(n.full + 1)[0:TP, 0:80], EPS, None, ALU.add).then_inc(psum_free, 1)
            dve.wait_ge(psum_free, n.free + 2)
            dve.tensor_scalar(s80[4][0:TP, :], s80[4][0:TP, :], 1.0, -1.0, ALU.min, ALU.max).then_inc(dve_out, 1)
            dve.wait_ge(act_out, n.a + 1)
            own(dve.tensor_tensor(s80[2][0:TP, :], s80[2][0:TP, :], s80[0][0:TP, :], ALU.mult))
            settle()
            skip(2, 2, 2)
            end()
            dve.wait_ge(psum_full, n.full + 1)
            own(dve.tensor_reduce(mtop[0:TP, 0:8], bank(n.full)[0:TP, 0:80].rearrange("p (t h) -> p h t", h=8),
                                  X_AXIS, ALU.add))
            settle()
            dve.sem_inc(psum_free, 1)
            own(dve.reciprocal(mtop[0:TP, 8:16], mtop[0:TP, 0:8]))
            settle()
            own(dve.scalar_tensor_tensor(s80[3][0:TP, :].rearrange("p (t h) -> p t h", h=8),
                                         s80[4][0:TP, :].rearrange("p (t h) -> p t h", h=8), float(N) / 8.0,
                                         mtop[0:TP, 8:16].unsqueeze(1).to_broadcast([TP, NT, 8]), ALU.mult, ALU.mult))
            settle()
            skip(1)
            end()
            for t in range(NT):
                dve.wait_ge(psum_full, n.full + t + 1)
                dve.tensor_tensor(heads(A2t[:, t, :]), heads(bank(n.full + t)[0:TP, :]), per_head(t, s80[3]), ALU.mult)\
                   .then_inc(psum_free, 1)
            skip(NT)
            add_rows(lambda t: MfA[:, t, :], lambda t: row("gnnA", 256))
            end()
            dve.wait_ge(psum_full, n.full + 1)
            dve.tensor_tensor(kvb, bank(n.full).rearrange("p (c e) -> p c e", c=KC),
                              mask_p[:, :].unsqueeze(1).to_broadcast([128, KC, 128]), ALU.mult).then_inc(psum_free, 1)
            skip(1)
            end()
            for t in range(NT):
                dve.wait_ge(psum_full, n.full + t + 1)
                dve.tensor_tensor(heads(R1t[:, t, :]), heads(bank(n.full + t)[0:TP, :]), per_head(t, s80[2]), ALU.mult)\
                   .then_inc(psum_free, 1)
            skip(NT)
            end()
            split_cols()
            end()
            own(dve.tensor_tensor(R2t, R2t, row("bproj").unsqueeze(1).to_broadcast([TP, NT, D]), ALU.add))
            settle()
            add_rows(lambda t: R2t[:, t, :], lambda t: R2t[:, t, :])
            dve.wait_ge(psum_free, n.free)
            end()
            own(dve.tensor_tensor(MfB, MfA, rinv[0:TP, :].unsqueeze(2).to_broadcast([TP, NT, 256]), ALU.mult))
            settle()
            skip(3)
            end()

            def msg_tail(q):
                c0, w = CH[q // 2]
                dve.wait_ge(act_out, n.a + q + 1)
                own(dve.tensor_tensor(XL[:, q % 2, c0:c0 + w], V[:, q % 4, 0:w],
                                      XH[:, q % 2, c0:c0 + w].bitcast(F32), ALU.subtract))

            for q in range(6):
                c0, w = CH[q // 2]
                dve.wait_ge(psum_full, n.full + q + 1)
                dve.tensor_tensor(V[:, q % 4, 0:w], bank(n.full + q)[:, 0:w], BC[:, 0, c0:c0 + w], ALU.mult)\
                   .then_inc(psum_free, 1)
                if q >= 1:
                    msg_tail(q - 1)
            msg_tail(5)
            for q in range(6, 12):
                c0, w = CH[q // 2 - 3]
                dve.wait_ge(act_out, n.a + q + 1)
                dve.tensor_tensor(XL[:, 2 + q % 2, c0:c0 + w], bank(n.full + q)[:, 0:w],
                                  XH[:, 2 + q % 2, c0:c0 + w].bitcast(F32), ALU.subtract).then_inc(psum_free, 1)
            skip(12, 12)
            end()
            add_rows(lambda t: hg[:, t, :], lambda t: row("gnnA", 128, 256))
            dve.wait_ge(psum_free, n.free)
            end()
            norm(hg, hg, 128, row("gnnA", 128, 384), row("gnnB", 128))
            own(dve.tensor_scalar(hg, hg, 0.0, None, ALU.max))
            settle()
            end()
            split_cols(1, HH, HL)
            end()
            for t in range(NT):
                v = V[0:TP, t % 4, :]
                dve.wait_ge(psum_full, n.full + t + 1)
                dve.tensor_tensor(v, bank(n.full + t)[0:TP, :], row("gnnb2"), ALU.add).then_inc(psum_free, 1)
                dve.wait_ge(psum_free, n.free + t + 1)
                own(dve.tensor_scalar(v, v, 0.0, valid[0:TP, t:t + 1], ALU.max, ALU.mult))
                settle()
                own(dve.tensor_tensor(R2t[:, t, :], R2t[:, t, :], v, ALU.add))
            settle()
            skip(NT)
            end()
            norm(R2t, R1t)
            end()
            split_cols()
            end()
            dve.wait_ge(psum_full, n.full + 1)
            dve.tensor_tensor(lg[0:TP, :].rearrange("p (t e) -> p t e", e=E1),
                              bank(n.full)[0:TP, 0:160].rearrange("p (t e) -> p t e", e=E1),
                              row("gnnB", E1, 128).unsqueeze(1).to_broadcast([TP, NT, E1]), ALU.add).then_inc(psum_free, 1)
            dve.wait_ge(psum_free, n.free + 1)
            skip(1)
            p3 = softmax(160, 2)
            l3 = lg[0:TP, :].rearrange("p (g e) -> p g e", e=8)
            g1 = gate[0:TP, :].unsqueeze(2).to_broadcast([TP, 2 * NT, 8])
            own(dve.tensor_reduce(gate[0:TP, :], p3, X_AXIS, ALU.max))
            settle()
            own(dve.tensor_tensor(l3, p3, g1, ALU.is_ge))
            settle()
            own(dve.tensor_tensor(l3, l3, iota8[0:TP, :].unsqueeze(1).to_broadcast([TP, 2 * NT, 8]), ALU.mult))
            settle()
            own(dve.tensor_reduce(mtop[0:TP, 0:20], l3, X_AXIS, ALU.max))
            settle()
            own(dve.tensor_tensor(l3, iota8[0:TP, :].unsqueeze(1).to_broadcast([TP, 2 * NT, 8]),
                                  mtop[0:TP, 0:20].unsqueeze(2).to_broadcast([TP, 2 * NT, 8]), ALU.is_equal))
            settle()
            own(dve.tensor_tensor(p3, l3, g1, ALU.mult))
            own(dve.tensor_tensor(R2t, R2t, row("bs2").unsqueeze(1).to_broadcast([TP, NT, D]), ALU.add))
            settle()
            end()
            skip(NT)
            end()
            add_rows(lambda t: R2t[:, t, :], lambda t: R2t[:, t, :])
            for e in range(1 + E1):
                for i in range(6):
                    c0, w = CH[i // 2]
                    dve.wait_ge(act_out, n.a + i + 1)
                    dve.tensor_tensor(HL[:, i % 2, c0:c0 + w], V[:, i % 4, 0:w], HH[:, i % 2, c0:c0 + w].bitcast(F32),
                                      ALU.subtract).then_inc(dve_out, 1)
                skip(6, 6, 6)
                if e == 0:
                    add_rows(lambda t: R2t[:, t, :], lambda t: R2t[:, t, :])
                else:
                    for t in range(NT):
                        dve.wait_ge(psum_full, n.full + t + 1)
                        dve.scalar_tensor_tensor(R2t[:, t, :], bank(n.full + t)[0:TP, :],
                                                 pr[0:TP, E1 * t + e - 1:E1 * t + e], R2t[:, t, :], ALU.mult, ALU.add)\
                           .then_inc(psum_free, 1)
                    skip(NT)



ROW_SLOT = {"bk": 0, "bv": 1, "bo": 2, "mg1": 3, "mbe1": 4, "mb2": 0, "mg2": 1, "mbe2": 2, "bp0": 3, "bl0": 4,
            "g0": 0, "be0": 1, "bp1": 2, "bl1": 3, "g1": 0, "be1": 1, "bp2": 4, "bl2": 2,
            "gnnA": 0, "gnnB": 1, "gnnb2": 3, "bproj": 2, "bs2": 4}


def lay_out(i):
    def chunks(w):
        k, m = w.shape
        return w.reshape(k // 128, 128, m).transpose(1, 0, 2).reshape(128, -1)

    def pair(w1, w2):
        return np.concatenate([chunks(w1), chunks(w2)], axis=1)

    g = np.concatenate([chunks(i["L1_gnn_Wm"]), chunks(i["L1_gnn_W1"]), chunks(i["L1_gnn_W2"])], axis=1)
    qkv = i["L1_mix_W_qkv"].T
    units = [chunks(i[f"L0_mix_W{k}"]) for k in "qkvo"] + [pair(i["L0_mix_W1"], i["L0_mix_W2"])]
    for l in range(3):
        units += [chunks(i[f"L0_gnn_W{k}{l}"].T) for k in "prl"]
    units += [pair(i["L0_ffn_W1"][e], i["L0_ffn_W2"][e]) for e in range(E0)]
    units += [chunks(qkv[:, D * k:D * k + D]) for k in range(3)]
    units += [g, chunks(i["L1_mix_W_proj"].T), g, pair(i["L1_ffn_Ws1"], i["L1_ffn_Ws2"])]
    for b in ("sp", "fq"):
        units += [pair(i[f"L1_ffn_W1_{b}"][e], i[f"L1_ffn_W2_{b}"][e]) for e in range(8)]
    f = "float32"
    gnn_a = np.concatenate([i["L1_gnn_bm"], i["L1_gnn_b1"], i["L1_gnn_gamma"]])
    gnn_b = np.concatenate([i["L1_gnn_beta"], i["L1_ffn_br_sp"], i["L1_ffn_br_fq"], np.zeros(368, f)])
    rows = {"bk": "L0_mix_bk", "bv": "L0_mix_bv", "bo": "L0_mix_bo", "mg1": "L0_mix_g1", "mbe1": "L0_mix_be1",
            "mb2": "L0_mix_b2", "mg2": "L0_mix_g2", "mbe2": "L0_mix_be2", "gnnb2": "L1_gnn_b2",
            "bproj": "L1_mix_b_proj", "bs2": "L1_ffn_bs2"}
    for l in range(3):
        rows[f"bp{l}"], rows[f"bl{l}"] = f"L0_gnn_bp{l}", f"L0_gnn_bl{l}"
    for l in range(2):
        rows[f"g{l}"], rows[f"be{l}"] = f"L0_gnn_g{l}", f"L0_gnn_be{l}"
    row_list = [gnn_a if r == "gnnA" else gnn_b if r == "gnnB" else i[rows[r]] for r in ROWS]
    cols = [i["L0_mix_bq"], i["L0_mix_b1"], i["L0_ffn_b1"], i["L1_ffn_bs1"], i["L1_ffn_b1_sp"], i["L1_ffn_b1_fq"]]
    return {
        "x": i["x"],
        "src": np.ascontiguousarray(i["src"].reshape(NCH, TP).T),
        "dst": np.ascontiguousarray(i["dst"].reshape(NCH, TP).T),
        "ew": np.ascontiguousarray(i["edge_weight"].reshape(NCH, TP).T),
        "units": np.stack(units),
        "rows": np.stack(row_list),
        "cols": np.ascontiguousarray(np.concatenate([c.reshape(-1, 128) for c in cols]).T),
        "wg": chunks(np.concatenate([i["L0_ffn_Wg"], i["L1_ffn_Wr_sp"], i["L1_ffn_Wr_fq"]], axis=1)),
        "b2f": i["L0_ffn_b2"],
        "b2e": np.concatenate([i["L1_ffn_b2_sp"], i["L1_ffn_b2_fq"]]),
    }


def kernel(**inputs):
    import concourse.bacc as _bacc
    from concourse.bass_utils import run_bass_kernel_spmd as _run

    nc = _bacc.Bacc("TRN2", target_bir_lowering=False, num_devices=1, dynamic_dma_scratch_size=1024)
    arrays, args = {}, {}
    for name, a in lay_out({k: np.asarray(v) for k, v in inputs.items()}).items():
        arrays[f"in_{name}"] = a
        args[name] = nc.dram_tensor(f"in_{name}", a.shape, mybir.dt.from_np(a.dtype), kind="ExternalInput").ap()
    out = nc.dram_tensor("out_0", (N, D), F32, kind="ExternalOutput").ap()
    program(nc, args, out)
    r = _run(nc, [arrays], core_ids=[0])
    return r.results[0]["out_0"]
```
